# Optimizing a Trainium2 kernel written in Bass

```python
import numpy as np
import jax
import jax.numpy as jnp

def _softmax(x, axis=-1):
    return jax.nn.softmax(x, axis=axis)

def _gelu(x):
    return jax.nn.gelu(x, approximate=True)

def _silu(x):
    return jax.nn.silu(x)

def _sigmoid(x):
    return jax.nn.sigmoid(x)

def _layernorm(x, axis=-1, eps=1e-05):
    m = jnp.mean(x, axis=axis, keepdims=True)
    v = jnp.var(x, axis=axis, keepdims=True)
    return (x - m) / jnp.sqrt(v + eps)

def _scatter_add(tgt, idx, src, axis=0):
    return tgt.at[idx].add(src)

def _segment_sum(src, seg, n):
    return jax.ops.segment_sum(src, seg, n)
kernel_name = 'mk_adaln_attn_ffn_d1_seqx_r8_3993b3'

def setup_inputs(seed: int=0):
    np.random.seed(seed)
    _w = jnp.asarray

    def _rec_inputs():
        import jax
        import jax.numpy as jnp
        _rk = jax.random.key(seed)
        x = -7.109e-05 + 0.9999 * jax.random.normal(jax.random.fold_in(_rk, 1), (8, 256, 128), jnp.float32)
        _lenS = 256 - jax.random.randint(jax.random.fold_in(_rk, 7), (8,), 0, max(1, 256 // 4) + 1, jnp.int32)
        _lenS2 = 256 - jax.random.randint(jax.random.fold_in(_rk, 8), (8,), 0, max(1, 256 // 4) + 1, jnp.int32)
        cond_512 = 0.0061147 + 1.02565 * jax.random.normal(jax.random.fold_in(_rk, 11), (8, 64), jnp.float32)
        return (x, cond_512)
    x, cond_512 = _rec_inputs()

    def _L0_cond_setup():
        import jax, jax.numpy as jnp
        import numpy as np
        W_DIM = 64
        CLAMP = 256.0
        key = jax.random.key(seed)
        ks = jax.random.split(key, 6)
        B, L, C = (8, 1024, 128)
        return {'x': jax.random.normal(ks[0], (B, L, C), dtype=jnp.float32), 'w': jax.random.normal(ks[1], (B, W_DIM), dtype=jnp.float32), 'weight': jax.random.normal(ks[2], (C, C), dtype=jnp.float32), 'bias': jax.random.normal(ks[3], (C,), dtype=jnp.float32), 'affine_w': jax.random.normal(ks[4], (C, W_DIM), dtype=jnp.float32), 'affine_b': jnp.ones((C,), dtype=jnp.float32)}
    _L0_cond_all = _L0_cond_setup()
    _L0_cond_in = {k: v for k, v in _L0_cond_all.items() if k in ('weight', 'bias', 'affine_w', 'affine_b')}
    del _L0_cond_all

    def _L0_attn_setup():
        import jax, jax.numpy as jnp
        import numpy as np
        import math
        N_HEAD = 16
        N_EMBD = 128
        HEAD_D = N_EMBD // N_HEAD
        BASE = 1250

        def rope(Y):
            d = Y.shape[-1]
            t = Y.shape[-2]
            theta = BASE ** (-2.0 * jnp.arange(d // 2, dtype=Y.dtype) / d)
            theta2 = jnp.concatenate([theta, theta], axis=0)
            pos = jnp.arange(1, t + 1, dtype=Y.dtype)
            C = pos[:, None] * theta2[None, :]
            cos, sin = (jnp.cos(C), jnp.sin(C))
            Y2 = jnp.concatenate([-Y[..., d // 2:], Y[..., :d // 2]], axis=-1)
            return Y * cos + Y2 * sin
        key = jax.random.key(seed)
        ks = jax.random.split(key, 9)
        s = 0.02
        x = jax.random.normal(ks[0], (4, 256, N_EMBD), dtype=jnp.float32)
        Wq = jax.random.normal(ks[1], (N_EMBD, N_EMBD), dtype=jnp.float32) * s
        bq = jnp.zeros((N_EMBD,), dtype=jnp.float32)
        Wk = jax.random.normal(ks[2], (N_EMBD, N_EMBD), dtype=jnp.float32) * s
        bk = jnp.zeros((N_EMBD,), dtype=jnp.float32)
        Wv = jax.random.normal(ks[3], (N_EMBD, N_EMBD), dtype=jnp.float32) * s
        bv = jnp.zeros((N_EMBD,), dtype=jnp.float32)
        Wo = jax.random.normal(ks[4], (N_EMBD, N_EMBD), dtype=jnp.float32) * s
        bo = jnp.zeros((N_EMBD,), dtype=jnp.float32)
        return {'x': x, 'Wq': Wq, 'bq': bq, 'Wk': Wk, 'bk': bk, 'Wv': Wv, 'bv': bv, 'Wo': Wo, 'bo': bo}
    _L0_attn_all = _L0_attn_setup()
    _L0_attn_in = {k: v for k, v in _L0_attn_all.items() if k in ('Wq', 'bq', 'Wk', 'bk', 'Wv', 'bv', 'Wo', 'bo')}
    del _L0_attn_all

    def _L0_cond2_setup():
        import jax, jax.numpy as jnp
        import numpy as np
        IN_DIM = 128
        OUT_DIM = 128
        MU_DIM = 64
        K = 30
        key = jax.random.key(seed)
        k1, k2, k3, k4, k5 = jax.random.split(key, 5)
        B, S = (16, 256)
        x = jax.random.normal(k1, (B, S, IN_DIM), dtype=jnp.float32)
        mu = jax.random.normal(k2, (B, MU_DIM), dtype=jnp.float32)
        W_dec = jax.random.normal(k3, (MU_DIM, (IN_DIM + 1) * K), dtype=jnp.float32) / np.sqrt(MU_DIM)
        b_dec = jax.random.normal(k4, ((IN_DIM + 1) * K,), dtype=jnp.float32) * 0.01
        V = jax.random.normal(k5, (K, OUT_DIM), dtype=jnp.float32) / np.sqrt(K)
        return {'x': x, 'mu': mu, 'W_dec': W_dec, 'b_dec': b_dec, 'V': V}
    _L0_cond2_all = _L0_cond2_setup()
    _L0_cond2_in = {k: v for k, v in _L0_cond2_all.items() if k in ('W_dec', 'b_dec', 'V')}
    del _L0_cond2_all

    def _L0_ffn_setup():
        import jax, jax.numpy as jnp
        import numpy as np

        def _binarize(w):
            alpha = jax.lax.stop_gradient(jnp.mean(jnp.abs(w), axis=1, keepdims=True))
            bw = alpha * jnp.sign(w)
            return w + jax.lax.stop_gradient(bw - w)
        key = jax.random.key(seed)
        k1, k2, k3, k4, k5 = jax.random.split(key, 5)
        D, H = (128, 512)
        x = jax.random.normal(k1, (64, 196, D), dtype=jnp.float32)
        w1 = jax.random.normal(k2, (H, D), dtype=jnp.float32) * 0.02
        b1 = jax.random.normal(k3, (H,), dtype=jnp.float32) * 0.02
        w2 = jax.random.normal(k4, (D, H), dtype=jnp.float32) * 0.02
        b2 = jax.random.normal(k5, (D,), dtype=jnp.float32) * 0.02
        return {'x': x, 'w1': w1, 'b1': b1, 'w2': w2, 'b2': b2}
    _L0_ffn_all = _L0_ffn_setup()
    _L0_ffn_in = {k: v for k, v in _L0_ffn_all.items() if k in ('w1', 'b1', 'w2', 'b2')}
    del _L0_ffn_all
    return {'x': x, 'cond_512': cond_512, 'L0_cond_weight': _L0_cond_in['weight'], 'L0_cond_bias': _L0_cond_in['bias'], 'L0_cond_affine_w': _L0_cond_in['affine_w'], 'L0_cond_affine_b': _L0_cond_in['affine_b'], 'L0_attn_Wq': _L0_attn_in['Wq'], 'L0_attn_bq': _L0_attn_in['bq'], 'L0_attn_Wk': _L0_attn_in['Wk'], 'L0_attn_bk': _L0_attn_in['bk'], 'L0_attn_Wv': _L0_attn_in['Wv'], 'L0_attn_bv': _L0_attn_in['bv'], 'L0_attn_Wo': _L0_attn_in['Wo'], 'L0_attn_bo': _L0_attn_in['bo'], 'L0_cond2_W_dec': _L0_cond2_in['W_dec'], 'L0_cond2_b_dec': _L0_cond2_in['b_dec'], 'L0_cond2_V': _L0_cond2_in['V'], 'L0_ffn_w1': _L0_ffn_in['w1'], 'L0_ffn_b1': _L0_ffn_in['b1'], 'L0_ffn_w2': _L0_ffn_in['w2'], 'L0_ffn_b2': _L0_ffn_in['b2']}

def reference(x, cond_512, L0_cond_weight, L0_cond_bias, L0_cond_affine_w, L0_cond_affine_b, L0_attn_Wq, L0_attn_bq, L0_attn_Wk, L0_attn_bk, L0_attn_Wv, L0_attn_bv, L0_attn_Wo, L0_attn_bo, L0_cond2_W_dec, L0_cond2_b_dec, L0_cond2_V, L0_ffn_w1, L0_ffn_b1, L0_ffn_w2, L0_ffn_b2):
    import jax
    import jax.numpy as jnp

    def _L0_cond_ref(x, w, weight, bias, affine_w, affine_b):
        import jax, jax.numpy as jnp
        import numpy as np
        W_DIM = 64
        CLAMP = 256.0
        B, L, C = x.shape
        gain = 1.0 / np.sqrt(W_DIM).astype(np.float32)
        styles = w @ (affine_w * gain).T + affine_b
        ws = weight[None, :, :] * styles[:, None, :]
        dcoefs = jax.lax.rsqrt(jnp.sum(ws * ws, axis=2) + 1e-08)
        xm = x * styles[:, None, :]
        y = jnp.einsum('blc,oc->blo', xm, weight)
        y = y * dcoefs[:, None, :]
        y = jnp.clip(y + bias, -CLAMP, CLAMP)
        return y

    def _L0_attn_ref(x, Wq, bq, Wk, bk, Wv, bv, Wo, bo):
        import jax, jax.numpy as jnp
        import numpy as np
        import math
        N_HEAD = 16
        N_EMBD = 128
        HEAD_D = N_EMBD // N_HEAD
        BASE = 1250

        def rope(Y):
            d = Y.shape[-1]
            t = Y.shape[-2]
            theta = BASE ** (-2.0 * jnp.arange(d // 2, dtype=Y.dtype) / d)
            theta2 = jnp.concatenate([theta, theta], axis=0)
            pos = jnp.arange(1, t + 1, dtype=Y.dtype)
            C = pos[:, None] * theta2[None, :]
            cos, sin = (jnp.cos(C), jnp.sin(C))
            Y2 = jnp.concatenate([-Y[..., d // 2:], Y[..., :d // 2]], axis=-1)
            return Y * cos + Y2 * sin
        b, t, _ = x.shape

        def split_heads(y):
            return y.reshape(b, t, N_HEAD, HEAD_D).transpose(0, 2, 1, 3)
        q = split_heads(x @ Wq.T + bq)
        k = split_heads(x @ Wk.T + bk)
        v = split_heads(x @ Wv.T + bv)
        q, k = (rope(q), rope(k))
        scale = math.sqrt(HEAD_D)
        att = jnp.einsum('bhqd,bhkd->bhqk', q, k) / scale
        mask = jnp.tril(jnp.ones((t, t), dtype=bool))
        att = jnp.where(mask, att, -jnp.inf)
        att = jax.nn.softmax(att, axis=-1)
        y = jnp.einsum('bhqk,bhkd->bhqd', att, v)
        y = y.transpose(0, 2, 1, 3).reshape(b, t, N_EMBD)
        return y @ Wo.T + bo

    def _L0_cond2_ref(x, mu, W_dec, b_dec, V):
        import jax, jax.numpy as jnp
        import numpy as np
        IN_DIM = 128
        OUT_DIM = 128
        MU_DIM = 64
        K = 30
        B = mu.shape[0]
        U = (mu @ W_dec + b_dec).reshape(B, IN_DIM + 1, K)
        param = jnp.einsum('bik,kj->bij', U, V)
        weight = param[:, :-1, :]
        bias = param[:, -1, :]
        out = jnp.einsum('bsd,bde->bse', x, weight)
        out = out + bias[:, None, :]
        return out

    def _L0_ffn_ref(x, w1, b1, w2, b2):
        import jax, jax.numpy as jnp
        import numpy as np

        def _binarize(w):
            alpha = jax.lax.stop_gradient(jnp.mean(jnp.abs(w), axis=1, keepdims=True))
            bw = alpha * jnp.sign(w)
            return w + jax.lax.stop_gradient(bw - w)
        bw1 = _binarize(w1)
        h = jnp.einsum('bsd,hd->bsh', x, bw1) + b1
        h = jax.nn.gelu(h, approximate=False)
        bw2 = _binarize(w2)
        out = jnp.einsum('bsh,dh->bsd', h, bw2) + b2
        return out
    x = x + _L0_attn_ref(_L0_cond_ref(x, cond_512, L0_cond_weight, L0_cond_bias, L0_cond_affine_w, L0_cond_affine_b), L0_attn_Wq, L0_attn_bq, L0_attn_Wk, L0_attn_bk, L0_attn_Wv, L0_attn_bv, L0_attn_Wo, L0_attn_bo)
    x = x + _L0_ffn_ref(_L0_cond2_ref(x, cond_512, L0_cond2_W_dec, L0_cond2_b_dec, L0_cond2_V), L0_ffn_w1, L0_ffn_b1, L0_ffn_w2, L0_ffn_b2)
    return x

_drawn_inputs = setup_inputs


def setup_inputs(seed=0):
    import zlib

    import numpy as np

    out = dict(_drawn_inputs(seed))
    spreads = {'L0_cond_affine_b': (1.0, 0.6),
     'L0_attn_bq': (0.0, 2.0),
     'L0_attn_bk': (0.0, 2.0),
     'L0_attn_bv': (0.0, 0.36),
     'L0_attn_bo': (0.0, 0.1)}
    factors = {'L0_cond_weight': 6.786,
     'L0_cond_affine_w': 8.0,
     'L0_attn_Wq': 8.0,
     'L0_attn_Wk': 8.0,
     'L0_cond2_b_dec': 8.0,
     'L0_ffn_b1': 8.0,
     'L0_ffn_b2': 3.163}
    for name, (base, spread) in spreads.items():
        noise = np.random.default_rng([zlib.crc32(name.encode()), seed]).standard_normal(out[name].shape)
        drawn = base * np.exp(spread * noise) if base else spread * noise
        out[name] = jnp.asarray(drawn.astype(out[name].dtype))
    for name, factor in factors.items():
        out[name] = (out[name] * factor).astype(out[name].dtype)
    return out
```

```python
from contextlib import ExitStack

import concourse.bass as bass
from concourse import mybir

ALU = mybir.AluOpType
ACT = mybir.ActivationFunctionType
AX = mybir.AxisListType
F32 = mybir.dt.float32
BF16 = mybir.dt.bfloat16

P = 128
B = 8
L = 256
T = L // P
C = 128
H = 16
D = C // H
W = 64
K = 30
F = 512
NF = F // P

SLOTS = 3
STACK = 6 * D
MROW = STACK
KST = 65
MASK0 = 65

V_BIAS, V_AFFB, V_BQ, V_BK, V_BV, V_BO, V_B2, V_B1 = 0, 1, 2, 3, 4, 5, 6, 7
NV = V_B1 + NF


def build(nc, xT, condT, affT, wT, wqkvT, woT, vecs, wdecT, bdec, bdecl, vmat, w1T, w2T,
          rope, rowsq, rowsk, zeros2, ident, identb, outT):
    with ExitStack() as ctx:
        def sb(name, shape, dt=F32):
            return ctx.enter_context(nc.sbuf_tensor(name, shape, dt))

        def sem(name):
            return ctx.enter_context(nc.semaphore(name))

        X = sb("X", [P, B * L])
        COND = sb("COND", [W, B])
        AFF = sb("AFF", [W, C])
        WM = sb("WM", [P, C])
        WQKV = sb("WQKV", [P, 3 * C])
        WO = sb("WO", [P, C])
        VEC = sb("VEC", [P, NV])
        WDEC = sb("WDEC", [W, K, C + 1])
        BDEC = sb("BDEC", [P, K])
        BDECL = sb("BDECL", [K, 1])
        VMAT = sb("VMAT", [P, C])
        W1 = sb("W1", [P, F])
        W2 = sb("W2", [P, NF, C])
        ROPE = sb("ROPE", [P, 2, L])
        ROWSQ = sb("ROWSQ", [P, P], BF16)
        ROWSK = sb("ROWSK", [P, P], BF16)
        ID = sb("ID", [P, P])
        IDB = sb("IDB", [P, P], BF16)
        STY = sb("STY", [P, B])
        STY2 = sb("STY2", [P, B])
        WM2 = sb("WM2", [P, C])
        DEM = sb("DEM", [P, 2, B])
        DCO = sb("DCO", [P, B])
        UDEC = sb("UDEC", [P, B, 32])
        UDECL = sb("UDECL", [K, B])
        UT = sb("UT", [P, 2, P])
        WB = sb("WB", [P, B, C])
        BB = sb("BB", [P, B])
        ABS1 = sb("ABS1", [P, F])
        ABS2 = sb("ABS2", [P, NF, C])
        SG1 = sb("SG1", [P, F])
        SG2 = sb("SG2", [P, NF, C])
        MEANC = sb("MEANC", [P, 2])
        ALPHA = sb("ALPHA", [P, NF + 1])
        XM = sb("XM", [P, 2, L])
        Y1 = sb("Y1", [P, L])
        Y = sb("Y", [P, 2, L])
        QK = sb("QK", [P, 2, L])
        RC = sb("RC", [P, 2, L])
        RS = sb("RS", [P, 2, L])
        RP = sb("RP", [P, 2, 2, L])
        PARTS = sb("PARTS", [P, 2, 3, L], BF16)
        REST = sb("REST", [P, 2, L])
        QS = [sb(f"QS{i}", [P, H, L], BF16) for i in range(SLOTS)]
        KS = [sb(f"KS{i}", [P, H, L], BF16) for i in range(SLOTS)]
        VA = [sb(f"VA{i}", [P, T, H, 32]) for i in range(4)]
        MX = sb("MX", [P, 2, T, H])
        MP = sb("MP", [P, 2, T, 2, 8], BF16)
        NM = sb("NM", [P, 2, L], BF16)
        PX = sb("PX", [P, 12, 1024])
        HS = PX[:, 0:4, :].rearrange("p (s m) (n t) -> p s (m n) t", s=2, n=2)
        O2 = PX[:, 4, :].rearrange("p (s t) -> p s t", s=2)
        OUT = PX[:, 5, :].rearrange("p (s t) -> p s t", s=2)
        OT = sb("OT", [P, 4, L])
        RL = sb("RL", [P, T, H])
        ON = sb("ON", [P, T, C])
        AT = sb("AT", [P, L])
        X1 = sb("X1", [P, B * L])
        FT = sb("FT", [P, 2, 2 * L])

        SCR = [nc.dram_tensor(f"parts{i}", [2, 3, P, L], BF16, kind="Internal").ap() for i in range(2)]

        PST = [ctx.enter_context(nc.psum_tensor(f"PST{i}", [P, 1024], F32)) for i in range(2)]
        PSM = [ctx.enter_context(nc.psum_tensor(f"PSM{i}", [P, 512], F32)) for i in range(2)]
        POUT = ctx.enter_context(nc.psum_tensor("POUT", [P, 512], F32))
        PIN = ctx.enter_context(nc.psum_tensor("PIN", [P, 512], F32))

        in_first = sem("in_first")
        in_x0 = sem("in_x0")
        in_x = sem("in_x")
        in_qkv = sem("in_qkv")
        in_rest = sem("in_rest")
        prep = sem("prep")
        prep_psum = sem("prep_psum")
        prep_act = sem("prep_act")
        rows_set = sem("rows_set")
        va_set = sem("va_set")
        xm_ready = sem("xm_ready")
        y_psum = sem("y_psum")
        y1_ready = sem("y1_ready")
        y_ready = sem("y_ready")
        qk_psum = sem("qk_psum")
        qk_sb = sem("qk_sb")
        v_psum = sem("v_psum")
        v_ready = sem("v_ready")
        rope_terms = sem("rope_terms")
        rope_ready = sem("rope_ready")
        part_made = sem("part_made")
        scratch = [sem(f"scratch{i}") for i in range(2)]
        stack = [sem(f"stack{i}") for i in range(SLOTS)]
        m_rows = [[sem(f"m_rows{i}{j}") for j in range(2)] for i in range(SLOTS)]
        smax_psum = sem("smax_psum")
        smax_read = sem("smax_read")
        m_hi = sem("m_hi")
        m_parts = sem("m_parts")
        m_psum = sem("m_psum")
        m_sb = sem("m_sb")
        st_psum = sem("st_psum")
        exp_done = sem("exp_done")
        mask_done = sem("mask_done")
        o_psum = sem("o_psum")
        o_sb = sem("o_sb")
        tr_psum = sem("tr_psum")
        rl_ready = sem("rl_ready")
        norm_done = sem("norm_done")
        at_psum = sem("at_psum")
        at_sb = sem("at_sb")
        wo_psum = sem("wo_psum")
        x1_ready = sem("x1_ready")
        dec_psum = sem("dec_psum")
        dec_sb = sem("dec_sb")
        abs_ready = sem("abs_ready")
        sign_ready = sem("sign_ready")
        o2_psum = sem("o2_psum")
        o2_sb = sem("o2_sb")
        h_psum = sem("h_psum")
        h_sb = sem("h_sb")
        f_psum = sem("f_psum")
        f_scaled = sem("f_scaled")
        out_ready = sem("out_ready")
        out_stored = [sem(f"out_stored{i}") for i in range(2)]

        def wait(eng, s, n):
            if n > 0:
                eng.wait_ge(s, n)

        N_FIRST, N_QKV, N_REST = 9, 2, 9
        STACKED = 6

        def stack_value(b):
            n = 0
            for bb in range(b % SLOTS, b + 1, SLOTS):
                n += 16 * (STACKED + (bb >= SLOTS))
            return n

        def unit_of(n):
            half, u = divmod(n, 6)
            return (half, 8 * half + 4 * u, 4, 0) if u < 2 else (half, 8 * half + 2 * (u - 2), 2, 1)

        block = ctx.enter_context(nc.Block())

        @block.sync
        def _(sp):
            for dst, src in ((COND[:, :], condT), (AFF[:, :], affT), (WM[:, :], wT), (VEC[:, :], vecs),
                             (ROWSQ[:, :], rowsq), (ROWSK[:, :], rowsk)):
                sp.dma_start(dst, src).then_inc(in_first, 16)
            sp.dma_start(X[:, 0:2 * L], xT[:, 0:2 * L]).then_inc(in_x0, 16)
            sp.dma_start(WQKV[:, :], wqkvT).then_inc(in_qkv, 16)
            sp.dma_start(ROPE[:, :, :], rope).then_inc(in_qkv, 16)
            sp.dma_start(ID[:, :], ident).then_inc(in_first, 16)
            sp.dma_start(IDB[:, :], identb).then_inc(in_first, 16)
            sp.dma_start(WO[:, :], woT).then_inc(in_first, 16)
            sp.dma_start(X[:, 2 * L:], xT[:, 2 * L:]).then_inc(in_x, 16)
            sp.dma_start(WDEC[:, :, :], wdecT).then_inc(in_rest, 16)
            sp.dma_start(BDEC[:, :], bdec).then_inc(in_rest, 16)
            sp.dma_start(BDECL[:, :], bdecl).then_inc(in_rest, 16)
            for j in range(4):
                sp.dma_start(VMAT[32 * j:32 * j + K, :], vmat).then_inc(in_rest, 16)
            sp.dma_start(W1[:, :], w1T).then_inc(in_rest, 16)
            sp.dma_start(W2[:, :, :], w2T).then_inc(in_rest, 16)

            def store_parts(b):
                sp.wait_ge(part_made, 4 * (b + 1))
                if b >= 2:
                    sp.wait_ge(stack[(b - 2) % SLOTS], stack_value(b - 2))
                sp.dma_start(SCR[b % 2].rearrange("s n p t -> p (s n) t"),
                             PARTS[:, :, :, :].rearrange("p s n t -> p (s n) t")) \
                    .then_inc(scratch[b % 2], 16)

            def stack_rows(b):
                s = b % SLOTS
                sp.wait_ge(scratch[b % 2], 16 * (b // 2 + 1))
                sp.wait_ge(rows_set, min(2 * (s + 1), 2 * SLOTS))
                if b >= SLOTS:
                    sp.wait_ge(st_psum, 6 * (b - SLOTS + 1))
                    sp.dma_start(QS[s][MROW:MROW + 2, :, :], zeros2).then_inc(stack[s], 16)
                q = SCR[b % 2][0].rearrange("n (d h) t -> (n d) (h t)", d=D)
                k = SCR[b % 2][1].rearrange("n (d h) t -> (n d) (h t)", d=D)
                sp.dma_start(QS[s][0:24, :, :].rearrange("p h t -> p (h t)"), q[0:24]).then_inc(stack[s], 16)
                sp.dma_start(QS[s][24:40, :, :].rearrange("p h t -> p (h t)"), q[0:16]).then_inc(stack[s], 16)
                sp.dma_start(QS[s][40:48, :, :].rearrange("p h t -> p (h t)"), q[0:8]).then_inc(stack[s], 16)
                sp.dma_start(KS[s][0:24, :, :].rearrange("p h t -> p (h t)"),
                             k[0:8].unsqueeze(0).to_broadcast([3, 8, H * L])).then_inc(stack[s], 16)
                sp.dma_start(KS[s][24:40, :, :].rearrange("p h t -> p (h t)"),
                             k[8:16].unsqueeze(0).to_broadcast([2, 8, H * L])).then_inc(stack[s], 16)
                sp.dma_start(KS[s][40:48, :, :].rearrange("p h t -> p (h t)"), k[16:24]).then_inc(stack[s], 16)

            def place_max(b, half):
                s = b % SLOTS
                sp.wait_ge(m_sb, 2 * b + half + 1)
                for part in range(2):
                    sp.dma_start(QS[s][MROW + part:MROW + part + 1, 8 * half:8 * half + 8, :],
                                 NM[8 * part:8 * part + 8, half, :]).then_inc(m_rows[s][half], 16)

            for s in range(-3, B + 1):
                if 0 <= s < B:
                    place_max(s, 1)
                if 0 <= s + 2 < B:
                    stack_rows(s + 2)
                if 0 <= s + 1 < B:
                    place_max(s + 1, 0)
                if 0 <= s + 3 < B:
                    store_parts(s + 3)
            for p in range(B // 2):
                sp.wait_ge(out_ready, p + 1)
                sp.dma_start(outT[:, 2 * L * p:2 * L * (p + 1)], OUT[:, p % 2, :]).then_inc(out_stored[p % 2], 16)
            for o in out_stored:
                sp.wait_ge(o, 16 * (B // 4))

        @block.tensor
        def _(pe):
            mm = pe.matmul

            pe.wait_ge(in_first, 16 * N_FIRST)
            mm(PIN[:, 0:B], AFF[:, :], COND[:, :], start=True, stop=True).then_inc(prep_psum, 1)
            pe.wait_ge(prep, 3)
            mm(PIN[:, B:2 * B], WM2[:, :], STY2[:, :], start=True, stop=True).then_inc(prep_psum, 1)

            def y_product(b):
                pe.wait_ge(xm_ready, b + 1)
                if b == 0:
                    pe.wait_ge(prep, 4)
                else:
                    pe.wait_ge(v_ready, b)
                    wait(pe, m_sb, 2 * (b - 3) + 1)
                mm(PIN[:, 0:L], WM[:, :], XM[:, b % 2, :], start=True, stop=True).then_inc(y_psum, 1)

            def qk_product(b):
                if b == 0:
                    pe.wait_ge(in_qkv, 16 * N_QKV)
                pe.wait_ge(y_ready, b + 1)
                wait(pe, m_sb, 2 * (b - 3) + 2)
                mm(PIN[:, 0:L], WQKV[:, 0:C], Y[:, b % 2, :], start=True, stop=True)
                mm(PIN[:, L:2 * L], WQKV[:, C:2 * C], Y[:, b % 2, :], start=True, stop=True) \
                    .then_inc(qk_psum, 1)

            def v_product(b):
                pe.wait_ge(qk_sb, 2 * (b + 1))
                for t in range(T):
                    m = mm(PIN[:, t * P:(t + 1) * P], Y[:, b % 2, t * P:(t + 1) * P], WQKV[:, 2 * C:],
                           start=True, stop=True)
                m.then_inc(v_psum, 1)

            def scores_for_max(b, n):
                s = b % SLOTS
                _, h0, nh, t = unit_of(n)
                if n == 0:
                    pe.wait_ge(stack[s], stack_value(b))
                wait(pe, smax_read, 12 * b + n - 1)
                out = PSM[n % 2]
                for i in range(nh):
                    h = h0 + i
                    q = slice(t * P, (t + 1) * P)
                    at = i * (t + 1) * P
                    if t:
                        mm(out[:, at:at + P], QS[s][0:KST, h, q], KS[s][0:KST, h, 0:P], start=True, stop=True)
                        at += P
                    m = mm(out[:, at:at + P], QS[s][:, h, q], KS[s][:, h, q], start=True, stop=True)
                m.then_inc(smax_psum, 1)

            def turn_max(b, half):
                pe.wait_ge(m_parts, 2 * b + half + 1)
                wait(pe, m_sb, 2 * b + half)
                if half == 0:
                    pe.wait_ge(v_ready, min(b + 3, B))
                else:
                    pe.wait_ge(y1_ready, min(b + 4, B))
                for t in range(T):
                    m = pe.transpose(PIN[0:16, 384 + 64 * t:448 + 64 * t].bitcast(BF16),
                                     MP[:, half, t, :, :].rearrange("p a h -> p (a h)"),
                                     IDB[:, :])
                m.then_inc(m_psum, 1)

            def scores(b, u):
                s = b % SLOTS
                half, w = divmod(u, 3)
                if w == 0:
                    pe.wait_ge(m_rows[s][half], 32 * (b // SLOTS + 1))
                wait(pe, exp_done, 6 * b + u - 1)
                out = PST[u % 2]
                if w < 2:
                    for i in range(4):
                        h = 8 * half + 4 * w + i
                        m = mm(out[:, i * L:(i + 1) * L], KS[s][0:KST, h, 0:P], QS[s][0:KST, h, :],
                               start=True, stop=True)
                else:
                    for i in range(8):
                        h = 8 * half + i
                        m = mm(out[:, i * P:(i + 1) * P], KS[s][0:KST, h, P:L], QS[s][0:KST, h, P:L],
                               start=True, stop=True)
                m.then_inc(st_psum, 1)

            def pv(b, half):
                if half == 0:
                    wait(pe, x1_ready, b)
                    pe.wait_ge(v_ready, b + 1)
                else:
                    pe.wait_ge(o_sb, 2 * b + 1)
                pe.wait_ge(mask_done, 6 * b + 3 * half + 3)
                px = 6 * (b % 2) + 3 * half
                for g in range(2):
                    for j in range(4):
                        h = 8 * half + 4 * g + j
                        mm(POUT[32 * j:32 * j + 32, g * L:(g + 1) * L], VA[b % 4][:, 0, h, :],
                           PX[:, px + g, j * L:(j + 1) * L], start=True, stop=False, skip_group_check=True)
                    for j in range(4):
                        h = 8 * half + 4 * g + j
                        m = mm(POUT[32 * j:32 * j + 32, g * L + P:(g + 1) * L], VA[b % 4][:, 1, h, :],
                               PX[:, px + 2, (4 * g + j) * P:(4 * g + j + 1) * P], start=False, stop=True,
                               skip_group_check=True)
                m.then_inc(o_psum, 1)

            def turn_out(b, t):
                pe.wait_ge(o_sb, 2 * b + 2)
                if t:
                    pe.wait_ge(norm_done, 2 * b + 1)
                for g in range(4):
                    m = pe.transpose(POUT[:, g * P:(g + 1) * P], OT[:, g, t * P:(t + 1) * P], ID[:, :])
                m.then_inc(tr_psum, 1)

            def turn_heads(b):
                pe.wait_ge(norm_done, 2 * b + 2)
                for t in range(T):
                    m = pe.transpose(POUT[:, t * P:(t + 1) * P], ON[:, t, :], ID[:, :])
                m.then_inc(at_psum, 1)

            def out_product(b):
                pe.wait_ge(at_sb, b + 1)
                mm(POUT[:, L:2 * L], WO[:, :], AT[:, :], start=True, stop=True).then_inc(wo_psum, 1)

            for s in range(-3, B + 1):
                front, big, now, tail = (0 <= x < B for x in (s + 3, s + 1, s, s - 1))
                for tick in range(12):
                    if now and tick == 2:
                        turn_max(s, 1)
                    if big:
                        scores_for_max(s + 1, tick)
                    if now and tick % 2 == 0:
                        scores(s, tick // 2)
                    if tick == 0 and front:
                        y_product(s + 3)
                    if tick == 1 and tail:
                        pv(s - 1, 1)
                    if tick == 3 and front:
                        qk_product(s + 3)
                    if tick == 4 and tail:
                        turn_out(s - 1, 0)
                    if tick == 5 and tail:
                        turn_out(s - 1, 1)
                    if tick == 6 and front:
                        v_product(s + 3)
                    if tick == 7 and tail:
                        turn_heads(s - 1)
                    if tick == 8 and big:
                        turn_max(s + 1, 0)
                    if tick == 9 and tail:
                        out_product(s - 1)
                    if tick == 11 and now:
                        pv(s, 0)

            pe.wait_ge(in_rest, 16 * N_REST)
            pe.wait_ge(exp_done, 6 * B)
            for k in range(K):
                mm(PST[0][:, k * B:(k + 1) * B], WDEC[:, k, 0:C], COND[:, :], start=True, stop=True)
            mm(PST[0][0:K, 512:512 + B], WDEC[:, :, C], COND[:, :], start=True, stop=True).then_inc(dec_psum, 1)
            pe.wait_ge(abs_ready, 2)
            pe.wait_ge(va_set, 11)
            pe.wait_ge(smax_read, 12 * B)
            for n in range(NF):
                mm(PSM[0][:, n:n + 1], ABS1[:, n * P:(n + 1) * P], MEANC[:, 0:1], start=True, stop=True)
            for n in range(NF):
                m = mm(PSM[1][:, 0:1], ABS2[:, n, :], MEANC[:, 1:2], start=(n == 0), stop=(n == NF - 1))
            m.then_inc(dec_psum, 1)
            pe.wait_ge(dec_sb, 2)
            for r in range(2):
                m = pe.transpose(PIN[:, r * P:(r + 1) * P],
                                 UDEC[:, 4 * r:4 * r + 4, :].rearrange("p b k -> p (b k)"), ID[:, :])
            m.then_inc(dec_psum, 1)
            pe.wait_ge(dec_sb, 5)
            for j in range(4):
                for r in range(2):
                    mm(PST[j // 2][:, 512 * (j % 2) + r * P:512 * (j % 2) + (r + 1) * P],
                       UT[32 * j:32 * j + K, r, :], VMAT[32 * j:32 * j + K, :], start=True, stop=True)
            mm(PSM[0][:, 256:256 + B], VMAT[0:K, :], UDECL[:, :], start=True, stop=True).then_inc(dec_psum, 1)

            def o2_product(p):
                if p == 0:
                    pe.wait_ge(dec_sb, 10)
                    pe.wait_ge(x1_ready, B)
                if p:
                    pe.wait_ge(o2_sb, 2 * p)
                for i in range(2):
                    b = 2 * p + i
                    m = mm(POUT[:, i * L:(i + 1) * L], WB[:, b, :], X1[:, b * L:(b + 1) * L],
                           start=True, stop=True)
                m.then_inc(o2_psum, 1)

            def h_products(p):
                pe.wait_ge(sign_ready, 2)
                pe.wait_ge(o2_sb, 2 * p + 2)
                for n in range(NF):
                    if p:
                        pe.wait_ge(h_sb, NF * (p - 1) + n + 1)
                    mm(PST[n // 2][:, 512 * (n % 2):512 * (n % 2) + 512], SG1[:, n * P:(n + 1) * P],
                       O2[:, p % 2, :], start=True, stop=True).then_inc(h_psum, 1)

            def f_products(p):
                wait(pe, f_scaled, p - 1)
                for n in range(NF):
                    pe.wait_ge(h_sb, NF * p + n + 1)
                    m = mm(PSM[p % 2][:, :], SG2[:, n, :], HS[:, p % 2, n, :], start=(n == 0),
                           stop=(n == NF - 1))
                m.then_inc(f_psum, 1)

            o2_product(0)
            h_products(0)
            for p in range(B // 2):
                if p + 1 < B // 2:
                    o2_product(p + 1)
                    h_products(p + 1)
                f_products(p)

        @block.scalar
        def _(act):
            def modulate(b):
                if b == 0:
                    act.wait_ge(in_x0, 16)
                    act.wait_ge(prep, 1)
                if b == 2:
                    act.wait_ge(in_x, 16)
                wait(act, y_psum, b - 1)
                nc.scalar.activation(XM[:, b % 2, :], X[:, b * L:(b + 1) * L], ACT.Copy,
                                     scale=STY[:, b:b + 1]).then_inc(xm_ready, 1)

            def demodulate(b):
                if b == 0:
                    act.wait_ge(prep, 5)
                act.wait_ge(y_psum, b + 1)
                wait(act, y_ready, b)
                nc.scalar.activation(Y1[:, :], PIN[:, 0:L], ACT.Identity, scale=DCO[:, b:b + 1],
                                     bias=VEC[:, V_BIAS:V_BIAS + 1]).then_inc(y1_ready, 1)

            def take_qk(b):
                act.wait_ge(qk_psum, b + 1)
                wait(act, rope_terms, 3 * b)
                for i, v in ((0, V_BQ), (1, V_BK)):
                    nc.scalar.activation(QK[:, i, :], PIN[:, i * L:(i + 1) * L], ACT.Identity,
                                         bias=VEC[:, v:v + 1]).then_inc(qk_sb, 1)

            def exponent(b, u):
                act.wait_ge(st_psum, 6 * b + u + 1)
                if b >= 2:
                    act.wait_ge(o_psum, 2 * (b - 2) + u // 3 + 1)
                nc.scalar.activation(PX[:, 6 * (b % 2) + u, :], PST[u % 2][:, :], ACT.Exp,
                                     scale=float(D) ** -0.5).then_inc(exp_done, 1)

            def take_out(b, half):
                act.wait_ge(o_psum, 2 * b + half + 1)
                wait(act, tr_psum, 2 * b)
                nc.scalar.activation(OT[:, 2 * half:2 * half + 2, :].rearrange("p g t -> p (g t)"),
                                     POUT[:, :], ACT.Copy).then_inc(o_sb, 1)

            def take_heads(b):
                act.wait_ge(at_psum, b + 1)
                wait(act, wo_psum, b)
                nc.scalar.activation(AT[:, :], POUT[:, 0:L], ACT.Identity,
                                     bias=VEC[:, V_BV:V_BV + 1]).then_inc(at_sb, 1)

            def take_max(b, half):
                act.wait_ge(m_psum, 2 * b + half + 1)
                if b:
                    act.wait_ge(m_rows[(b - 1) % SLOTS][half], 32 * ((b - 1) // SLOTS + 1))
                nc.scalar.activation(NM[0:16, half, :], PIN[0:16, 384:512].bitcast(BF16), ACT.Copy) \
                    .then_inc(m_sb, 1)

            act.wait_ge(prep, 4)
            nc.scalar.activation(DEM[:, 1, :], DEM[:, 0, :], ACT.Sqrt).then_inc(prep_act, 1)
            for s in range(-3, B + 1):
                front, big, now, tail = (0 <= x < B for x in (s + 3, s + 1, s, s - 1))
                for tick in range(12):
                    if tick == 0 and front:
                        modulate(s + 3)
                        demodulate(s + 3)
                    if now and tick % 2 == 0:
                        if tick == 2:
                            take_max(s, 1)
                        exponent(s, tick // 2)
                    if tick == 2 and tail:
                        take_out(s - 1, 1)
                    if tick == 4 and front:
                        take_qk(s + 3)
                    if tick == 8 and tail:
                        take_heads(s - 1)
                    if tick == 9 and big:
                        take_max(s + 1, 0)
                    if tick == 11 and now:
                        take_out(s, 0)

            act.wait_ge(in_rest, 16 * N_REST)
            nc.scalar.activation(ABS1[:, :], W1[:, :], ACT.Abs).then_inc(abs_ready, 1)
            nc.scalar.activation(ABS2[:, :, :], W2[:, :, :], ACT.Abs).then_inc(abs_ready, 1)
            nc.scalar.activation(SG1[:, :], W1[:, :], ACT.Sign).then_inc(sign_ready, 1)
            nc.scalar.activation(SG2[:, :, :], W2[:, :, :], ACT.Sign).then_inc(sign_ready, 1)
            act.wait_ge(dec_sb, 4)
            for p in range(B // 2):
                for n in range(NF):
                    act.wait_ge(h_psum, NF * p + n + 1)
                    wait(act, f_psum, p - 1)
                    nc.scalar.activation(HS[:, p % 2, n, :], PST[n // 2][:, 512 * (n % 2):512 * (n % 2) + 512],
                                         ACT.Gelu, scale=ALPHA[:, n:n + 1],
                                         bias=VEC[:, V_B1 + n:V_B1 + n + 1]).then_inc(h_sb, 1)

        @block.gpsimd
        def _(pool):
            for i in range(4):
                pool.memset(VA[i][:, :, :, D:32], 0.0).then_inc(va_set, 1)
            pool.memset(UDEC[:, :, K:32], 0.0).then_inc(va_set, 1)
            pool.memset(MEANC[:, 0:1], 1.0 / C).then_inc(va_set, 1)
            pool.memset(MEANC[:, 1:2], 1.0 / F).then_inc(va_set, 1)
            pool.wait_ge(va_set, 7)
            for i in range(4):
                pool.memset(VA[i][:, :, :, D:D + 1], 1.0).then_inc(va_set, 1)

            def split(b):
                src = RP[:, b % 2, :, :]
                pool.wait_ge(rope_ready, b + 1)
                wait(pool, scratch[(b - 1) % 2], 16 * ((b - 1) // 2 + 1) if b else 0)
                pool.tensor_scalar(PARTS[:, :, 0, :], src, 1.0, 1.0, ALU.mult, ALU.mult).then_inc(part_made, 1)
                pool.wait_ge(part_made, 4 * b + 1)
                pool.tensor_tensor(REST[:, :, :], src, PARTS[:, :, 0, :], ALU.subtract).then_inc(part_made, 1)
                pool.wait_ge(part_made, 4 * b + 2)
                pool.tensor_scalar(PARTS[:, :, 1, :], REST[:, :, :], 1.0, 1.0, ALU.mult, ALU.mult) \
                    .then_inc(part_made, 1)
                pool.wait_ge(part_made, 4 * b + 3)
                pool.tensor_tensor(PARTS[:, :, 2, :], REST[:, :, :], PARTS[:, :, 1, :], ALU.subtract) \
                    .then_inc(part_made, 1)

            def causal(b, u):
                pool.wait_ge(exp_done, 6 * b + u + 1)
                px = PX[:, 6 * (b % 2) + u, :]
                if u % 3 < 2:
                    v, n = px.rearrange("p (h q) -> p h q", h=4)[:, :, 0:P], 4
                else:
                    v, n = px.rearrange("p (h q) -> p h q", h=8), 8
                pool.affine_select(out=v, in_=v, compare_op=ALU.is_ge, fill=0.0, base=0,
                                   pattern=[[0, n], [1, P]], channel_multiplier=-1).then_inc(mask_done, 1)

            for s in range(-3, B + 1):
                front, now = 0 <= s + 3 < B, 0 <= s < B
                for tick in range(12):
                    if now and tick % 2 == 1:
                        causal(s, tick // 2)
                    if tick == 8 and front:
                        split(s + 3)

        @block.vector
        def _(dve):
            v = nc.vector
            dve.wait_ge(prep_psum, 1)
            v.tensor_scalar(STY[:, :], PIN[:, 0:B], float(W) ** -0.5, VEC[:, V_AFFB:V_AFFB + 1],
                            ALU.mult, ALU.add).then_inc(prep, 1)
            dve.wait_ge(prep, 1)
            v.tensor_tensor(STY2[:, :], STY[:, :], STY[:, :], ALU.mult).then_inc(prep, 1)
            v.tensor_tensor(WM2[:, :], WM[:, :], WM[:, :], ALU.mult).then_inc(prep, 1)
            dve.wait_ge(prep_psum, 2)
            v.tensor_scalar(DEM[:, 0, :], PIN[:, B:2 * B], 1e-8, None, ALU.add).then_inc(prep, 1)
            dve.wait_ge(prep_act, 1)
            v.reciprocal(DCO[:, :], DEM[:, 1, :]).then_inc(prep, 1)

            def set_rows(i):
                for S, R in ((QS, ROWSQ), (KS, ROWSK)):
                    v.tensor_copy(S[i][:, :, :].rearrange("p h (t q) -> p (h t) q", q=P),
                                  R[:, :].unsqueeze(1).to_broadcast([P, H * T, P])).then_inc(rows_set, 1)

            def clip(b):
                dve.wait_ge(y1_ready, b + 1)
                wait(dve, v_psum, b - 1)
                v.tensor_scalar(Y[:, b % 2, :], Y1[:, :], 256.0, -256.0, ALU.min, ALU.max) \
                    .then_inc(y_ready, 1)

            def take_v(b):
                if b == 0:
                    dve.wait_ge(va_set, 11)
                dve.wait_ge(v_psum, b + 1)
                wait(dve, o_psum, 2 * (b - 4) + 2)
                v.tensor_copy(VA[b % 4][:, :, :, 0:D], PIN[:, 0:L].rearrange("p (t h d) -> p t h d", t=T, d=D)) \
                    .then_inc(v_ready, 1)

            def rope(b):
                if b == 0:
                    dve.wait_ge(in_qkv, 16 * N_QKV)
                dve.wait_ge(qk_sb, 2 * b + 2)
                cos = ROPE[:, 0, :].unsqueeze(1).to_broadcast([P, 2, L])
                sin = ROPE[:, 1, :].unsqueeze(1).to_broadcast([P, 2, L])
                wait(dve, rope_ready, b)
                v.tensor_tensor(RS[0:64, :, :], QK[64:128, :, :], sin[64:128], ALU.mult).then_inc(rope_terms, 1)
                v.tensor_tensor(RS[64:128, :, :], QK[0:64, :, :], sin[0:64], ALU.mult).then_inc(rope_terms, 1)
                v.tensor_tensor(RC[:, :, :], QK[:, :, :], cos, ALU.mult).then_inc(rope_terms, 1)
                dve.wait_ge(rope_terms, 3 * b + 3)
                wait(dve, part_made, 4 * (b - 1))
                v.tensor_tensor(RP[:, b % 2, :, :], RC[:, :, :], RS[:, :, :], ALU.add).then_inc(rope_ready, 1)

            def reduce_max(b, n):
                _, h0, nh, t = unit_of(n)
                dve.wait_ge(smax_psum, 12 * b + n + 1)
                if n == 0:
                    wait(dve, m_parts, 2 * (b - 1))
                v.tensor_reduce(MX[:, b % 2, t, h0:h0 + nh],
                                PSM[n % 2][:, :].rearrange("p (h k) -> p h k", h=nh), AX.X, ALU.max) \
                    .then_inc(smax_read, 1)

            def split_max(b, half):
                dve.wait_ge(smax_read, 12 * b + 6 * half + 6)
                wait(dve, m_psum, 2 * (b - 1) + half + 1)
                mx = MX[:, b % 2, :, 8 * half:8 * half + 8]
                v.tensor_scalar(MP[:, half, :, 0, :], mx, -1.0, None, ALU.mult).then_inc(m_hi, 1)
                dve.wait_ge(m_hi, 2 * b + half + 1)
                v.scalar_tensor_tensor(out=MP[:, half, :, 1, :], in0=mx, scalar=-1.0,
                                       in1=MP[:, half, :, 0, :], op0=ALU.mult, op1=ALU.subtract) \
                    .then_inc(m_parts, 1)

            def normalise(b, t):
                dve.wait_ge(tr_psum, 2 * b + t + 1)
                wait(dve, at_psum, b)
                o = POUT[:, :].rearrange("p (h c) -> p h c", c=32)
                v.reciprocal(RL[:, t, :], o[:, :, D]).then_inc(rl_ready, 1)
                dve.wait_ge(rl_ready, 2 * b + t + 1)
                v.tensor_tensor(ON[:, t, :].rearrange("p (h d) -> p h d", d=D), o[:, :, 0:D],
                                RL[:, t, :].unsqueeze(2).to_broadcast([P, H, D]), ALU.mult) \
                    .then_inc(norm_done, 1)

            def residual(b):
                dve.wait_ge(wo_psum, b + 1)
                v.scalar_tensor_tensor(out=X1[:, b * L:(b + 1) * L], in0=POUT[:, L:2 * L],
                                       scalar=VEC[:, V_BO:V_BO + 1], in1=X[:, b * L:(b + 1) * L],
                                       op0=ALU.add, op1=ALU.add).then_inc(x1_ready, 1)

            for s in range(-3, B + 1):
                front, big, now, tail = (0 <= x < B for x in (s + 3, s + 1, s, s - 1))
                for tick in range(12):
                    if tick == 1 and now:
                        split_max(s, 1)
                    if big:
                        reduce_max(s + 1, tick)
                    if tick == 1 and front:
                        clip(s + 3)
                        if s < 0:
                            set_rows(s + 3)
                    if tick == 5 and front:
                        rope(s + 3)
                    if tick in (5, 6) and tail:
                        normalise(s - 1, tick - 5)
                    if tick == 7 and front:
                        take_v(s + 3)
                    if tick == 7 and big:
                        split_max(s + 1, 0)
                    if tick == 10 and tail:
                        residual(s - 1)

            dve.wait_ge(in_rest, 16 * N_REST)
            dve.wait_ge(dec_psum, 1)
            v.tensor_tensor(UDEC[:, :, 0:K], PST[0][:, 0:K * B].rearrange("p (k b) -> p b k", b=B),
                            BDEC[:, :].unsqueeze(1).to_broadcast([P, B, K]), ALU.add).then_inc(dec_sb, 1)
            v.tensor_scalar(UDECL[:, :], PST[0][0:K, 512:512 + B], BDECL[:, 0:1], None, ALU.add) \
                .then_inc(dec_sb, 1)
            dve.wait_ge(dec_psum, 2)
            v.tensor_copy(ALPHA[:, 0:NF], PSM[0][:, 0:NF]).then_inc(dec_sb, 1)
            v.tensor_copy(ALPHA[:, NF:NF + 1], PSM[1][:, 0:1]).then_inc(dec_sb, 1)
            dve.wait_ge(dec_psum, 3)
            v.tensor_copy(UT[:, :, :], PIN[:, 0:2 * P].rearrange("p (r i) -> p r i", r=2)).then_inc(dec_sb, 1)
            dve.wait_ge(dec_psum, 4)
            for j in range(4):
                v.tensor_copy(WB[:, j:B:4, :],
                              PST[j // 2][:, 512 * (j % 2):512 * (j % 2) + 2 * P]
                              .rearrange("p (r e) -> p r e", r=2)).then_inc(dec_sb, 1)
            v.tensor_copy(BB[:, :], PSM[0][:, 256:256 + B]).then_inc(dec_sb, 1)

            def take_o2(p):
                dve.wait_ge(o2_psum, p + 1)
                if p == 0:
                    dve.wait_ge(dec_sb, 10)
                wait(dve, h_psum, NF * (p - 1))
                for i in range(2):
                    b = 2 * p + i
                    v.tensor_scalar(O2[:, p % 2, i * L:(i + 1) * L], POUT[:, i * L:(i + 1) * L],
                                    BB[:, b:b + 1], None, ALU.add).then_inc(o2_sb, 1)

            def finish(p):
                dve.wait_ge(f_psum, p + 1)
                v.tensor_scalar(FT[:, p % 2, :], PSM[p % 2][:, :], ALPHA[:, NF:NF + 1],
                                VEC[:, V_B2:V_B2 + 1], ALU.mult, ALU.add).then_inc(f_scaled, 1)
                dve.wait_ge(f_scaled, p + 1)
                wait(dve, out_stored[p % 2], 16 * (p // 2))
                v.tensor_tensor(OUT[:, p % 2, :], FT[:, p % 2, :], X1[:, 2 * L * p:2 * L * (p + 1)],
                                ALU.add).then_inc(out_ready, 1)

            take_o2(0)
            for p in range(B // 2):
                if p + 1 < B // 2:
                    take_o2(p + 1)
                finish(p)


def kernel(**inputs):
    import numpy as np
    import concourse.bacc as bacc
    from concourse.bass_utils import run_bass_kernel_spmd as run

    a = {k: np.asarray(v) for k, v in inputs.items()}
    bf = np.dtype("bfloat16")

    order = np.arange(C).reshape(H, D).T.reshape(-1)
    wq, wk = a["L0_attn_Wq"][order], a["L0_attn_Wk"][order]

    theta = np.float32(1250) ** (np.float32(-2.0) * np.arange(D // 2, dtype=np.float32) / np.float32(D))
    theta = np.concatenate([theta, theta]).astype(np.float32)
    angle = np.arange(1, L + 1, dtype=np.float32)[None, :] * np.repeat(theta, H)[:, None]
    sign = np.where(np.arange(C) < C // 2, 1.0, -1.0).astype(np.float32)[:, None]
    rope = np.stack([np.cos(angle), sign * np.sin(angle)], axis=1).astype(np.float32)
    rowsq, rowsk = np.zeros((P, P)), np.zeros((P, P))
    rowsk[MROW:MROW + 2] = 1.0
    i = np.arange(P)
    for r in range(32):
        rowsq[MASK0 + r] = np.where(i // 4 == r, 2.0 ** (-42.0 * (i % 4)), 0.0)
        rowsk[MASK0 + r] = np.where(i // 4 == r, -(2.0 ** (-12 + 42.0 * (i % 4))), 0.0)
    for r in range(1, 32):
        rowsq[MASK0 + 31 + r] = i // 4 < r
        rowsk[MASK0 + 31 + r] = np.where(i // 4 == r, -(2.0 ** 60), 0.0)

    col = lambda v: v.reshape(-1, P).T
    vecs = np.concatenate([col(a["L0_cond_bias"]), col(a["L0_cond_affine_b"]), col(a["L0_attn_bq"][order]),
                           col(a["L0_attn_bk"][order]), col(a["L0_attn_bv"]), col(a["L0_attn_bo"]),
                           col(a["L0_ffn_b2"]), col(a["L0_ffn_b1"])], axis=1)
    bdec = a["L0_cond2_b_dec"].reshape(C + 1, K)
    arrays = {
        "xT": a["x"].reshape(B * L, C).T,
        "condT": a["cond_512"].T,
        "affT": a["L0_cond_affine_w"].T,
        "wT": a["L0_cond_weight"].T,
        "wqkvT": np.concatenate([wq, wk, a["L0_attn_Wv"]], axis=0).T,
        "woT": a["L0_attn_Wo"].T,
        "vecs": vecs,
        "wdecT": a["L0_cond2_W_dec"].reshape(W, C + 1, K).transpose(0, 2, 1),
        "bdec": bdec[:C],
        "bdecl": bdec[C:].T,
        "vmat": a["L0_cond2_V"],
        "w1T": a["L0_ffn_w1"].T,
        "w2T": a["L0_ffn_w2"].T.reshape(NF, P, C).transpose(1, 0, 2),
        "rope": rope,
        "rowsq": rowsq.astype(bf),
        "rowsk": rowsk.astype(bf),
        "zeros2": np.zeros((2, H, L), bf),
        "ident": np.eye(P, dtype=np.float32),
        "identb": np.eye(P).astype(bf),
    }
    arrays = {k: np.ascontiguousarray(v) for k, v in arrays.items()}
    nc = bacc.Bacc("TRN2", target_bir_lowering=False, num_devices=1)
    args = [nc.dram_tensor(k, v.shape, mybir.dt.from_np(v.dtype), kind="ExternalInput").ap()
            for k, v in arrays.items()]
    out = nc.dram_tensor("outT", (C, B * L), F32, kind="ExternalOutput").ap()
    build(nc, *args, out)
    r = run(nc, [arrays], core_ids=[0])
    return r.results[0]["outT"].T.reshape(B, L, C)
```

```python
from contextlib import ExitStack

import concourse.bass as bass
from concourse import mybir

ALU = mybir.AluOpType
ACT = mybir.ActivationFunctionType
AX = mybir.AxisListType
F32 = mybir.dt.float32
BF16 = mybir.dt.bfloat16

P = 128
B = 8
L = 256
T = L // P
C = 128
H = 16
D = C // H
W = 64
K = 30
F = 512
NF = F // P

SLOTS = 3
STACK = 6 * D
MROW = STACK
KST = 65
MASK0 = 65

V_BIAS, V_AFFB, V_BQ, V_BK, V_BV, V_BO, V_B2, V_B1 = 0, 1, 2, 3, 4, 5, 6, 7
NV = V_B1 + NF


def build(nc, xT, condT, affT, wT, wqkvT, woT, vecs, wdecT, bdec, bdecl, vmat, w1T, w2T,
          rope, rowsq, rowsk, zeros2, ident, identb, outT):
    with ExitStack() as ctx:
        def sb(name, shape, dt=F32):
            return ctx.enter_context(nc.sbuf_tensor(name, shape, dt))

        def sem(name):
            return ctx.enter_context(nc.semaphore(name))

        X = sb("X", [P, B * L])
        COND = sb("COND", [W, B])
        AFF = sb("AFF", [W, C])
        WM = sb("WM", [P, C])
        WQKV = sb("WQKV", [P, 3 * C])
        WO = sb("WO", [P, C])
        VEC = sb("VEC", [P, NV])
        WDEC = sb("WDEC", [W, K, C + 1])
        BDEC = sb("BDEC", [P, K])
        BDECL = sb("BDECL", [K, 1])
        VMAT = sb("VMAT", [P, C])
        W1 = sb("W1", [P, F])
        W2 = sb("W2", [P, NF, C])
        ROPE = sb("ROPE", [P, 2, L])
        ROWSQ = sb("ROWSQ", [P, P], BF16)
        ROWSK = sb("ROWSK", [P, P], BF16)
        ID = sb("ID", [P, P])
        IDB = sb("IDB", [P, P], BF16)
        STY = sb("STY", [P, B])
        STY2 = sb("STY2", [P, B])
        WM2 = sb("WM2", [P, C])
        DEM = sb("DEM", [P, 2, B])
        DCO = sb("DCO", [P, B])
        UDEC = sb("UDEC", [P, B, 32])
        UDECL = sb("UDECL", [K, B])
        UT = sb("UT", [P, 2, P])
        WB = sb("WB", [P, B, C])
        BB = sb("BB", [P, B])
        ABS1 = sb("ABS1", [P, F])
        ABS2 = sb("ABS2", [P, NF, C])
        SG1 = sb("SG1", [P, F])
        SG2 = sb("SG2", [P, NF, C])
        MEANC = sb("MEANC", [P, 2])
        ALPHA = sb("ALPHA", [P, NF + 1])
        XM = sb("XM", [P, 2, L])
        Y1 = sb("Y1", [P, L])
        Y = sb("Y", [P, 2, L])
        QK = sb("QK", [P, 2, L])
        RC = sb("RC", [P, 2, L])
        RS = sb("RS", [P, 2, L])
        RP = sb("RP", [P, 2, 2, L])
        PARTS = sb("PARTS", [P, 2, 3, L], BF16)
        REST = sb("REST", [P, 2, L])
        QS = [sb(f"QS{i}", [P, H, L], BF16) for i in range(SLOTS)]
        KS = [sb(f"KS{i}", [P, H, L], BF16) for i in range(SLOTS)]
        VA = [sb(f"VA{i}", [P, T, H, 32]) for i in range(4)]
        MX = sb("MX", [P, 2, T, H])
        MP = sb("MP", [P, 2, T, 2, 8], BF16)
        NM = sb("NM", [P, 2, L], BF16)
        PX = sb("PX", [P, 12, 1024])
        HS = PX[:, 0:4, :].rearrange("p (s m) (n t) -> p s (m n) t", s=2, n=2)
        O2 = PX[:, 4, :].rearrange("p (s t) -> p s t", s=2)
        OUT = PX[:, 5, :].rearrange("p (s t) -> p s t", s=2)
        OT = sb("OT", [P, 4, L])
        RL = sb("RL", [P, T, H])
        ON = sb("ON", [P, T, C])
        AT = sb("AT", [P, L])
        X1 = sb("X1", [P, B * L])
        FT = sb("FT", [P, 2, 2 * L])

        SCR = [nc.dram_tensor(f"parts{i}", [2, 3, P, L], BF16, kind="Internal").ap() for i in range(2)]

        PST = [ctx.enter_context(nc.psum_tensor(f"PST{i}", [P, 512], F32)) for i in range(3)]
        PSM = [ctx.enter_context(nc.psum_tensor(f"PSM{i}", [P, 512], F32)) for i in range(3)]
        POUT = ctx.enter_context(nc.psum_tensor("POUT", [P, 512], F32))
        PIN = ctx.enter_context(nc.psum_tensor("PIN", [P, 512], F32))
        PH = [PST[0], PST[1], PST[2], PSM[0]]
        PF = [PSM[1], PSM[2]]
        PWB = [PST[0], PST[1], PST[2], PSM[2]]

        in_first = sem("in_first")
        in_x0 = sem("in_x0")
        in_x = sem("in_x")
        in_qkv = sem("in_qkv")
        in_rest = sem("in_rest")
        prep = sem("prep")
        prep_psum = sem("prep_psum")
        prep_act = sem("prep_act")
        rows_set = sem("rows_set")
        va_set = sem("va_set")
        xm_ready = sem("xm_ready")
        y_psum = sem("y_psum")
        y1_ready = sem("y1_ready")
        y_ready = sem("y_ready")
        qk_psum = sem("qk_psum")
        qk_sb = sem("qk_sb")
        v_psum = sem("v_psum")
        v_ready = sem("v_ready")
        rope_terms = sem("rope_terms")
        rope_cos = sem("rope_cos")
        rope_ready = sem("rope_ready")
        part1_made = sem("part1_made")
        part_made = sem("part_made")
        scratch = [sem(f"scratch{i}") for i in range(2)]
        stack = [sem(f"stack{i}") for i in range(SLOTS)]
        m_rows = [[sem(f"m_rows{i}{j}") for j in range(2)] for i in range(SLOTS)]
        smax_psum = sem("smax_psum")
        smax_read = sem("smax_read")
        m_hi = sem("m_hi")
        m_parts = sem("m_parts")
        m_psum = sem("m_psum")
        m_sb = sem("m_sb")
        st_psum = sem("st_psum")
        exp_done = sem("exp_done")
        mask_done = sem("mask_done")
        o_psum = sem("o_psum")
        o_sb = sem("o_sb")
        tr_psum = sem("tr_psum")
        rl_ready = sem("rl_ready")
        norm_done = sem("norm_done")
        at_psum = sem("at_psum")
        at_sb = sem("at_sb")
        wo_psum = sem("wo_psum")
        x1_ready = sem("x1_ready")
        dec_psum = sem("dec_psum")
        dec_sb = sem("dec_sb")
        abs_ready = sem("abs_ready")
        sign_ready = sem("sign_ready")
        o2_psum = sem("o2_psum")
        o2_sb = sem("o2_sb")
        h_psum = sem("h_psum")
        h_sb = sem("h_sb")
        f_psum = sem("f_psum")
        f_scaled = sem("f_scaled")
        out_ready = sem("out_ready")
        out_stored = [sem(f"out_stored{i}") for i in range(2)]

        def wait(eng, s, n):
            if n > 0:
                eng.wait_ge(s, n)

        N_FIRST, N_QKV, N_REST = 9, 2, 9
        N_DEC = 9
        STACKED = 6

        def stack_value(b):
            n = 0
            for bb in range(b % SLOTS, b + 1, SLOTS):
                n += 16 * (STACKED + (bb >= SLOTS))
            return n

        def unit_of(n):
            half, u = divmod(n, 6)
            return (half, 8 * half + 4 * u, 4, 0) if u < 2 else (half, 8 * half + 2 * (u - 2), 2, 1)

        block = ctx.enter_context(nc.Block())

        @block.sync
        def _(sp):
            for dst, src in ((COND[:, :], condT), (AFF[:, :], affT), (WM[:, :], wT), (VEC[:, :], vecs),
                             (ROWSQ[:, :], rowsq), (ROWSK[:, :], rowsk)):
                sp.dma_start(dst, src).then_inc(in_first, 16)
            sp.dma_start(X[:, 0:2 * L], xT[:, 0:2 * L]).then_inc(in_x0, 16)
            sp.dma_start(WQKV[:, :], wqkvT).then_inc(in_qkv, 16)
            sp.dma_start(ROPE[:, :, :], rope).then_inc(in_qkv, 16)
            sp.dma_start(ID[:, :], ident).then_inc(in_first, 16)
            sp.dma_start(IDB[:, :], identb).then_inc(in_first, 16)
            sp.dma_start(WO[:, :], woT).then_inc(in_first, 16)
            sp.dma_start(X[:, 2 * L:], xT[:, 2 * L:]).then_inc(in_x, 16)
            sp.dma_start(WDEC[:, :, :], wdecT).then_inc(in_rest, 16)
            sp.dma_start(BDEC[:, :], bdec).then_inc(in_rest, 16)
            sp.dma_start(BDECL[:, :], bdecl).then_inc(in_rest, 16)
            for j in range(4):
                sp.dma_start(VMAT[32 * j:32 * j + K, :], vmat).then_inc(in_rest, 16)
            sp.dma_start(W1[:, :], w1T).then_inc(in_rest, 16)
            sp.dma_start(W2[:, :, :], w2T).then_inc(in_rest, 16)

            def store_parts(b):
                sp.wait_ge(part_made, 3 * (b + 1))
                if b >= 2:
                    sp.wait_ge(stack[(b - 2) % SLOTS], stack_value(b - 2))
                sp.dma_start(SCR[b % 2].rearrange("s n p t -> p (s n) t"),
                             PARTS[:, :, :, :].rearrange("p s n t -> p (s n) t")) \
                    .then_inc(scratch[b % 2], 16)

            def stack_rows(b):
                s = b % SLOTS
                sp.wait_ge(scratch[b % 2], 16 * (b // 2 + 1))
                sp.wait_ge(rows_set, min(2 * (s + 1), 2 * SLOTS))
                if b >= SLOTS:
                    sp.wait_ge(st_psum, 12 * (b - SLOTS + 1))
                    sp.dma_start(QS[s][MROW:MROW + 2, :, :], zeros2).then_inc(stack[s], 16)
                q = SCR[b % 2][0].rearrange("n (d h) t -> (n d) (h t)", d=D)
                k = SCR[b % 2][1].rearrange("n (d h) t -> (n d) (h t)", d=D)
                sp.dma_start(QS[s][0:24, :, :].rearrange("p h t -> p (h t)"), q[0:24]).then_inc(stack[s], 16)
                sp.dma_start(QS[s][24:40, :, :].rearrange("p h t -> p (h t)"), q[0:16]).then_inc(stack[s], 16)
                sp.dma_start(QS[s][40:48, :, :].rearrange("p h t -> p (h t)"), q[0:8]).then_inc(stack[s], 16)
                sp.dma_start(KS[s][0:24, :, :].rearrange("p h t -> p (h t)"),
                             k[0:8].unsqueeze(0).to_broadcast([3, 8, H * L])).then_inc(stack[s], 16)
                sp.dma_start(KS[s][24:40, :, :].rearrange("p h t -> p (h t)"),
                             k[8:16].unsqueeze(0).to_broadcast([2, 8, H * L])).then_inc(stack[s], 16)
                sp.dma_start(KS[s][40:48, :, :].rearrange("p h t -> p (h t)"), k[16:24]).then_inc(stack[s], 16)

            def place_max(b, half):
                s = b % SLOTS
                sp.wait_ge(m_sb, 2 * b + half + 1)
                for part in range(2):
                    sp.dma_start(QS[s][MROW + part:MROW + part + 1, 8 * half:8 * half + 8, :],
                                 NM[8 * part:8 * part + 8, half, :]).then_inc(m_rows[s][half], 16)

            for s in range(-3, B + 1):
                if 0 <= s < B:
                    place_max(s, 1)
                if 0 <= s + 2 < B:
                    stack_rows(s + 2)
                if 0 <= s + 1 < B:
                    place_max(s + 1, 0)
                if 0 <= s + 3 < B:
                    store_parts(s + 3)
            for p in range(B // 2):
                sp.wait_ge(out_ready, p + 1)
                sp.dma_start(outT[:, 2 * L * p:2 * L * (p + 1)], OUT[:, p % 2, :]).then_inc(out_stored[p % 2], 16)
            for o in out_stored:
                sp.wait_ge(o, 16 * (B // 4))

        @block.tensor
        def _(pe):
            mm = pe.matmul

            pe.wait_ge(in_first, 16 * N_FIRST)
            mm(PIN[:, 0:B], AFF[:, :], COND[:, :], start=True, stop=True).then_inc(prep_psum, 1)
            pe.wait_ge(prep, 3)
            mm(PIN[:, B:2 * B], WM2[:, :], STY2[:, :], start=True, stop=True).then_inc(prep_psum, 1)

            def y_product(b):
                pe.wait_ge(xm_ready, b + 1)
                if b == 0:
                    pe.wait_ge(prep, 4)
                else:
                    pe.wait_ge(v_ready, b)
                    wait(pe, m_sb, 2 * (b - 3) + 2)
                mm(PIN[:, 0:L], WM[:, :], XM[:, b % 2, :], start=True, stop=True).then_inc(y_psum, 1)

            def qk_product(b):
                if b == 0:
                    pe.wait_ge(in_qkv, 16 * N_QKV)
                pe.wait_ge(y_ready, b + 1)
                mm(PIN[:, 0:L], WQKV[:, 0:C], Y[:, b % 2, :], start=True, stop=True)
                mm(PIN[:, L:2 * L], WQKV[:, C:2 * C], Y[:, b % 2, :], start=True, stop=True) \
                    .then_inc(qk_psum, 1)

            def v_product(b):
                pe.wait_ge(qk_sb, 2 * (b + 1))
                wait(pe, m_sb, 2 * (b - 2) + 1)
                for t in range(T):
                    m = mm(PIN[:, t * P:(t + 1) * P], Y[:, b % 2, t * P:(t + 1) * P], WQKV[:, 2 * C:],
                           start=True, stop=True)
                m.then_inc(v_psum, 1)

            def scores_for_max(b, n):
                s = b % SLOTS
                _, h0, nh, t = unit_of(n)
                if n == 0:
                    pe.wait_ge(stack[s], stack_value(b))
                if b == 0 and n == 2:
                    pe.wait_ge(dec_sb, N_DEC)
                wait(pe, smax_read, 12 * b + n - 2)
                out = PSM[(12 * b + n) % 3]
                for i in range(nh):
                    h = h0 + i
                    q = slice(t * P, (t + 1) * P)
                    at = i * (t + 1) * P
                    if t:
                        mm(out[:, at:at + P], QS[s][0:KST, h, q], KS[s][0:KST, h, 0:P], start=True, stop=True)
                        at += P
                    m = mm(out[:, at:at + P], QS[s][:, h, q], KS[s][:, h, q], start=True, stop=True)
                m.then_inc(smax_psum, 1)

            def turn_max(b, half):
                pe.wait_ge(m_parts, 2 * b + half + 1)
                wait(pe, m_sb, 2 * b + half)
                if half == 0:
                    pe.wait_ge(qk_sb, 2 * min(b + 3, B))
                else:
                    pe.wait_ge(v_ready, min(b + 3, B))
                for t in range(T):
                    m = pe.transpose(PIN[0:16, 384 + 64 * t:448 + 64 * t].bitcast(BF16),
                                     MP[:, half, t, :, :].rearrange("p a h -> p (a h)"),
                                     IDB[:, :])
                m.then_inc(m_psum, 1)

            def scores(b, u):
                s = b % SLOTS
                half, w = divmod(u, 6)
                if w == 0:
                    pe.wait_ge(m_rows[s][half], 32 * (b // SLOTS + 1))
                if b == 0 and u == 0:
                    pe.wait_ge(dec_sb, N_DEC)
                wait(pe, exp_done, 12 * b + u - 2)
                out = PST[(12 * b + u) % 3]
                if w < 4:
                    for i in range(2):
                        h = 8 * half + 2 * w + i
                        m = mm(out[:, i * L:(i + 1) * L], KS[s][0:KST, h, 0:P], QS[s][0:KST, h, :],
                               start=True, stop=True)
                else:
                    for i in range(4):
                        h = 8 * half + 4 * (w - 4) + i
                        m = mm(out[:, i * P:(i + 1) * P], KS[s][0:KST, h, P:L], QS[s][0:KST, h, P:L],
                               start=True, stop=True)
                m.then_inc(st_psum, 1)

            def pv(b, half):
                if half == 0:
                    wait(pe, x1_ready, b)
                    pe.wait_ge(v_ready, b + 1)
                else:
                    pe.wait_ge(o_sb, 2 * b + 1)
                pe.wait_ge(mask_done, 6 * b + 3 * half + 3)
                px = 6 * (b % 2) + 3 * half
                for g in range(2):
                    for j in range(4):
                        h = 8 * half + 4 * g + j
                        mm(POUT[32 * j:32 * j + 32, g * L:(g + 1) * L], VA[b % 4][:, 0, h, :],
                           PX[:, px + g, j * L:(j + 1) * L], start=True, stop=False, skip_group_check=True)
                    for j in range(4):
                        h = 8 * half + 4 * g + j
                        m = mm(POUT[32 * j:32 * j + 32, g * L + P:(g + 1) * L], VA[b % 4][:, 1, h, :],
                               PX[:, px + 2, (4 * g + j) * P:(4 * g + j + 1) * P], start=False, stop=True,
                               skip_group_check=True)
                m.then_inc(o_psum, 1)

            def turn_out(b, t):
                pe.wait_ge(o_sb, 2 * b + 2)
                if t:
                    pe.wait_ge(norm_done, 2 * b + 1)
                for g in range(4):
                    m = pe.transpose(POUT[:, g * P:(g + 1) * P], OT[:, g, t * P:(t + 1) * P], ID[:, :])
                m.then_inc(tr_psum, 1)

            def turn_heads(b):
                pe.wait_ge(norm_done, 2 * b + 2)
                for t in range(T):
                    m = pe.transpose(POUT[:, t * P:(t + 1) * P], ON[:, t, :], ID[:, :])
                m.then_inc(at_psum, 1)

            def out_product(b):
                pe.wait_ge(at_sb, b + 1)
                mm(POUT[:, L:2 * L], WO[:, :], AT[:, :], start=True, stop=True).then_inc(wo_psum, 1)

            def decode():
                pe.wait_ge(in_rest, 16 * N_REST)
                for k in range(K):
                    mm(PST[0][:, k * B:(k + 1) * B], WDEC[:, k, 0:C], COND[:, :], start=True, stop=True)
                mm(PST[0][0:K, K * B:K * B + B], WDEC[:, :, C], COND[:, :], start=True, stop=True) \
                    .then_inc(dec_psum, 1)
                pe.wait_ge(abs_ready, 2)
                pe.wait_ge(va_set, 11)
                for n in range(NF):
                    mm(PST[1][:, n:n + 1], ABS1[:, n * P:(n + 1) * P], MEANC[:, 0:1], start=True, stop=True)
                for n in range(NF):
                    m = mm(PST[1][:, NF:NF + 1], ABS2[:, n, :], MEANC[:, 1:2], start=(n == 0),
                           stop=(n == NF - 1))
                m.then_inc(dec_psum, 1)

            def decode_turn():
                pe.wait_ge(dec_sb, 2)
                for r in range(2):
                    m = pe.transpose(PST[2][:, r * P:(r + 1) * P],
                                     UDEC[:, 4 * r:4 * r + 4, :].rearrange("p b k -> p (b k)"), ID[:, :])
                m.then_inc(dec_psum, 1)

            def decode_weights():
                pe.wait_ge(dec_sb, 4)
                for j in range(4):
                    for r in range(2):
                        mm(PWB[j][:, r * P:(r + 1) * P], UT[32 * j:32 * j + K, r, :],
                           VMAT[32 * j:32 * j + K, :], start=True, stop=True)
                mm(PST[0][:, 256:256 + B], VMAT[0:K, :], UDECL[:, :], start=True, stop=True) \
                    .then_inc(dec_psum, 1)

            for s in range(-3, B):
                front, big, now, tail = (0 <= x < B for x in (s + 3, s + 1, s, s - 1))
                for tick in range(12):
                    if tick == 1 and now:
                        turn_max(s, 1)
                    if big:
                        scores_for_max(s + 1, tick)
                    if now:
                        scores(s, tick)
                    if tick == 2 and front:
                        y_product(s + 3)
                    if tick == 2 and tail:
                        pv(s - 1, 1)
                    if tick == 4 and front:
                        qk_product(s + 3)
                    if tick == 4 and tail:
                        turn_out(s - 1, 0)
                    if tick == 6 and tail:
                        turn_out(s - 1, 1)
                    if tick == 7 and big:
                        turn_max(s + 1, 0)
                    if tick == 8 and front:
                        v_product(s + 3)
                    if tick == 8 and tail:
                        turn_heads(s - 1)
                    if tick == 10 and tail:
                        out_product(s - 1)
                    if tick == 11 and now:
                        pv(s, 0)
                if s == -3:
                    decode()
                if s == -2:
                    decode_turn()
                    decode_weights()

            def o2_product(p):
                if p == 0:
                    pe.wait_ge(m_sb, 2 * B)
                else:
                    pe.wait_ge(o2_sb, 2 * p)
                pe.wait_ge(x1_ready, 2 * p + 2)
                for i in range(2):
                    b = 2 * p + i
                    m = mm(PIN[:, i * L:(i + 1) * L], WB[:, b, :], X1[:, b * L:(b + 1) * L],
                           start=True, stop=True)
                m.then_inc(o2_psum, 1)

            def h_products(p):
                if p == 0:
                    pe.wait_ge(sign_ready, 2)
                    pe.wait_ge(exp_done, 12 * B)
                    pe.wait_ge(smax_read, 12 * B)
                pe.wait_ge(o2_sb, 2 * p + 2)
                for n in range(NF):
                    wait(pe, h_sb, NF * (p - 1) + n + 1 if p else 0)
                    mm(PH[n][:, :], SG1[:, n * P:(n + 1) * P], O2[:, p % 2, :], start=True, stop=True) \
                        .then_inc(h_psum, 1)

            def f_products(p):
                wait(pe, f_scaled, p - 1)
                for n in range(NF):
                    pe.wait_ge(h_sb, NF * p + n + 1)
                    m = mm(PF[p % 2][:, :], SG2[:, n, :], HS[:, p % 2, n, :], start=(n == 0),
                           stop=(n == NF - 1))
                m.then_inc(f_psum, 1)

            o2_product(0)
            pv(B - 1, 1)
            h_products(0)
            turn_out(B - 1, 0)
            o2_product(1)
            h_products(1)
            turn_out(B - 1, 1)
            f_products(0)
            turn_heads(B - 1)
            o2_product(2)
            h_products(2)
            out_product(B - 1)
            f_products(1)
            o2_product(3)
            h_products(3)
            f_products(2)
            f_products(3)

        @block.scalar
        def _(act):
            def modulate(b):
                if b == 0:
                    act.wait_ge(in_x0, 16)
                    act.wait_ge(prep, 1)
                if b == 2:
                    act.wait_ge(in_x, 16)
                wait(act, y_psum, b - 1)
                nc.scalar.activation(XM[:, b % 2, :], X[:, b * L:(b + 1) * L], ACT.Copy,
                                     scale=STY[:, b:b + 1]).then_inc(xm_ready, 1)

            def demodulate(b):
                if b == 0:
                    act.wait_ge(prep, 5)
                act.wait_ge(y_psum, b + 1)
                wait(act, y_ready, b)
                nc.scalar.activation(Y1[:, :], PIN[:, 0:L], ACT.Identity, scale=DCO[:, b:b + 1],
                                     bias=VEC[:, V_BIAS:V_BIAS + 1]).then_inc(y1_ready, 1)

            def take_qk(b):
                act.wait_ge(qk_psum, b + 1)
                wait(act, rope_terms, 2 * b)
                wait(act, rope_cos, b)
                for i, v in ((0, V_BQ), (1, V_BK)):
                    nc.scalar.activation(QK[:, i, :], PIN[:, i * L:(i + 1) * L], ACT.Identity,
                                         bias=VEC[:, v:v + 1]).then_inc(qk_sb, 1)

            def part1(b):
                act.wait_ge(rope_ready, b + 1)
                if b:
                    act.wait_ge(scratch[(b - 1) % 2], 16 * ((b - 1) // 2 + 1))
                nc.scalar.activation(PARTS[:, :, 0, :], RP[:, b % 2, :, :], ACT.Copy).then_inc(part1_made, 1)

            def take_v(b):
                if b == 0:
                    act.wait_ge(va_set, 11)
                act.wait_ge(v_psum, b + 1)
                wait(act, o_psum, 2 * (b - 4) + 2)
                nc.scalar.activation(VA[b % 4][:, :, :, 0:D],
                                     PIN[:, 0:L].rearrange("p (t h d) -> p t h d", t=T, d=D),
                                     ACT.Copy).then_inc(v_ready, 1)

            def exponent(b, u):
                act.wait_ge(st_psum, 12 * b + u + 1)
                if b >= 2:
                    act.wait_ge(o_psum, 2 * (b - 2) + u // 6 + 1)
                nc.scalar.activation(PX[:, 6 * (b % 2) + u // 2, 512 * (u % 2):512 * (u % 2) + 512],
                                     PST[(12 * b + u) % 3][:, :], ACT.Exp, scale=float(D) ** -0.5) \
                    .then_inc(exp_done, 1)

            def take_out(b, half):
                act.wait_ge(o_psum, 2 * b + half + 1)
                wait(act, tr_psum, 2 * b)
                nc.scalar.activation(OT[:, 2 * half:2 * half + 2, :].rearrange("p g t -> p (g t)"),
                                     POUT[:, :], ACT.Copy).then_inc(o_sb, 1)

            def take_heads(b):
                act.wait_ge(at_psum, b + 1)
                wait(act, wo_psum, b)
                nc.scalar.activation(AT[:, :], POUT[:, 0:L], ACT.Identity,
                                     bias=VEC[:, V_BV:V_BV + 1]).then_inc(at_sb, 1)

            def take_max(b, half):
                act.wait_ge(m_psum, 2 * b + half + 1)
                if b:
                    act.wait_ge(m_rows[(b - 1) % SLOTS][half], 32 * ((b - 1) // SLOTS + 1))
                nc.scalar.activation(NM[0:16, half, :], PIN[0:16, 384:512].bitcast(BF16), ACT.Copy) \
                    .then_inc(m_sb, 1)

            act.wait_ge(prep, 4)
            nc.scalar.activation(DEM[:, 1, :], DEM[:, 0, :], ACT.Sqrt).then_inc(prep_act, 1)
            for s in range(-3, B):
                front, big, now, tail = (0 <= x < B for x in (s + 3, s + 1, s, s - 1))
                for tick in range(12):
                    if tick == 0 and tail:
                        take_out(s - 1, 0)
                    if tick == 1 and front:
                        modulate(s + 3)
                    if tick == 2 and now:
                        take_max(s, 1)
                    if tick == 3 and front:
                        demodulate(s + 3)
                    if tick == 3 and tail:
                        take_out(s - 1, 1)
                    if tick == 5 and front:
                        take_qk(s + 3)
                    if tick == 8 and big:
                        take_max(s + 1, 0)
                    if tick == 9 and tail:
                        take_heads(s - 1)
                    if tick == 9 and front:
                        take_v(s + 3)
                        part1(s + 3)
                    if now:
                        exponent(s, tick)
                if s == -3:
                    act.wait_ge(in_rest, 16 * N_REST)
                    nc.scalar.activation(ABS1[:, :], W1[:, :], ACT.Abs).then_inc(abs_ready, 1)
                    nc.scalar.activation(ABS2[:, :, :], W2[:, :, :], ACT.Abs).then_inc(abs_ready, 1)
                    nc.scalar.activation(SG1[:, :], W1[:, :], ACT.Sign).then_inc(sign_ready, 1)
                    nc.scalar.activation(SG2[:, :, :], W2[:, :, :], ACT.Sign).then_inc(sign_ready, 1)

            def hidden(p, n):
                act.wait_ge(h_psum, NF * p + n + 1)
                wait(act, f_psum, p - 1)
                nc.scalar.activation(HS[:, p % 2, n, :], PH[n][:, :], ACT.Gelu, scale=ALPHA[:, n:n + 1],
                                     bias=VEC[:, V_B1 + n:V_B1 + n + 1]).then_inc(h_sb, 1)

            take_out(B - 1, 0)
            take_out(B - 1, 1)
            act.wait_ge(dec_sb, N_DEC)
            for p in range(B // 2):
                for n in range(NF):
                    hidden(p, n)
                if p == 1:
                    take_heads(B - 1)

        @block.gpsimd
        def _(pool):
            for i in range(4):
                pool.memset(VA[i][:, :, :, D:32], 0.0).then_inc(va_set, 1)
            pool.memset(UDEC[:, :, K:32], 0.0).then_inc(va_set, 1)
            pool.memset(MEANC[:, 0:1], 1.0 / C).then_inc(va_set, 1)
            pool.memset(MEANC[:, 1:2], 1.0 / F).then_inc(va_set, 1)
            pool.wait_ge(va_set, 7)
            for i in range(4):
                pool.memset(VA[i][:, :, :, D:D + 1], 1.0).then_inc(va_set, 1)

            def cosine(b):
                if b == 0:
                    pool.wait_ge(in_qkv, 16 * N_QKV)
                pool.wait_ge(qk_sb, 2 * b + 2)
                wait(pool, rope_ready, b)
                pool.tensor_tensor(RC[:, :, :], QK[:, :, :], ROPE[:, 0, :].unsqueeze(1).to_broadcast([P, 2, L]),
                                   ALU.mult).then_inc(rope_cos, 1)

            def split(b):
                pool.wait_ge(part1_made, b + 1)
                pool.tensor_tensor(REST[:, :, :], RP[:, b % 2, :, :], PARTS[:, :, 0, :], ALU.subtract) \
                    .then_inc(part_made, 1)
                pool.wait_ge(part_made, 3 * b + 1)
                pool.tensor_scalar(PARTS[:, :, 1, :], REST[:, :, :], 1.0, 1.0, ALU.mult, ALU.mult) \
                    .then_inc(part_made, 1)
                pool.wait_ge(part_made, 3 * b + 2)
                pool.tensor_tensor(PARTS[:, :, 2, :], REST[:, :, :], PARTS[:, :, 1, :], ALU.subtract) \
                    .then_inc(part_made, 1)

            def causal(b, u):
                pool.wait_ge(exp_done, 12 * b + 2 * u + 2)
                px = PX[:, 6 * (b % 2) + u, :]
                if u % 3 < 2:
                    v, n = px.rearrange("p (h q) -> p h q", h=4)[:, :, 0:P], 4
                else:
                    v, n = px.rearrange("p (h q) -> p h q", h=8), 8
                pool.affine_select(out=v, in_=v, compare_op=ALU.is_ge, fill=0.0, base=0,
                                   pattern=[[0, n], [1, P]], channel_multiplier=-1).then_inc(mask_done, 1)

            for s in range(-3, B):
                front, now = 0 <= s + 3 < B, 0 <= s < B
                for tick in range(12):
                    if tick == 6 and front:
                        cosine(s + 3)
                    if tick == 10 and front:
                        split(s + 3)
                    if now and tick % 2 == 1:
                        causal(s, tick // 2)

        @block.vector
        def _(dve):
            v = nc.vector
            dve.wait_ge(prep_psum, 1)
            v.tensor_scalar(STY[:, :], PIN[:, 0:B], float(W) ** -0.5, VEC[:, V_AFFB:V_AFFB + 1],
                            ALU.mult, ALU.add).then_inc(prep, 1)
            dve.wait_ge(prep, 1)
            v.tensor_tensor(STY2[:, :], STY[:, :], STY[:, :], ALU.mult).then_inc(prep, 1)
            v.tensor_tensor(WM2[:, :], WM[:, :], WM[:, :], ALU.mult).then_inc(prep, 1)
            dve.wait_ge(prep_psum, 2)
            v.tensor_scalar(DEM[:, 0, :], PIN[:, B:2 * B], 1e-8, None, ALU.add).then_inc(prep, 1)
            dve.wait_ge(prep_act, 1)
            v.reciprocal(DCO[:, :], DEM[:, 1, :]).then_inc(prep, 1)

            def set_rows(i):
                for S, R in ((QS, ROWSQ), (KS, ROWSK)):
                    v.tensor_copy(S[i][:, :, :].rearrange("p h (t q) -> p (h t) q", q=P),
                                  R[:, :].unsqueeze(1).to_broadcast([P, H * T, P])).then_inc(rows_set, 1)

            def clip(b):
                dve.wait_ge(y1_ready, b + 1)
                wait(dve, v_psum, b - 1)
                v.tensor_scalar(Y[:, b % 2, :], Y1[:, :], 256.0, -256.0, ALU.min, ALU.max) \
                    .then_inc(y_ready, 1)

            def rope_sine(b, side):
                if b == 0:
                    dve.wait_ge(in_qkv, 16 * N_QKV)
                dve.wait_ge(qk_sb, 2 * b + 2)
                wait(dve, rope_ready, b)
                a, o = (64, 0) if side == 0 else (0, 64)
                v.tensor_tensor(RS[o:o + 64, :, :], QK[a:a + 64, :, :],
                                ROPE[a:a + 64, 1, :].unsqueeze(1).to_broadcast([64, 2, L]), ALU.mult) \
                    .then_inc(rope_terms, 1)

            def rope_sum(b):
                dve.wait_ge(rope_terms, 2 * b + 2)
                dve.wait_ge(rope_cos, b + 1)
                wait(dve, part_made, 3 * (b - 1))
                v.tensor_tensor(RP[:, b % 2, :, :], RC[:, :, :], RS[:, :, :], ALU.add).then_inc(rope_ready, 1)

            def reduce_max(b, n):
                _, h0, nh, t = unit_of(n)
                dve.wait_ge(smax_psum, 12 * b + n + 1)
                if n == 0:
                    wait(dve, m_parts, 2 * (b - 1))
                v.tensor_reduce(MX[:, b % 2, t, h0:h0 + nh],
                                PSM[(12 * b + n) % 3][:, :].rearrange("p (h k) -> p h k", h=nh), AX.X, ALU.max) \
                    .then_inc(smax_read, 1)

            def split_max(b, half):
                dve.wait_ge(smax_read, 12 * b + 6 * half + 6)
                wait(dve, m_psum, 2 * (b - 1) + half + 1)
                mx = MX[:, b % 2, :, 8 * half:8 * half + 8]
                v.tensor_scalar(MP[:, half, :, 0, :], mx, -1.0, None, ALU.mult).then_inc(m_hi, 1)
                dve.wait_ge(m_hi, 2 * b + half + 1)
                v.scalar_tensor_tensor(out=MP[:, half, :, 1, :], in0=mx, scalar=-1.0,
                                       in1=MP[:, half, :, 0, :], op0=ALU.mult, op1=ALU.subtract) \
                    .then_inc(m_parts, 1)

            def normalise(b, t):
                dve.wait_ge(tr_psum, 2 * b + t + 1)
                wait(dve, at_psum, b)
                o = POUT[:, :].rearrange("p (h c) -> p h c", c=32)
                v.reciprocal(RL[:, t, :], o[:, :, D]).then_inc(rl_ready, 1)
                dve.wait_ge(rl_ready, 2 * b + t + 1)
                v.tensor_tensor(ON[:, t, :].rearrange("p (h d) -> p h d", d=D), o[:, :, 0:D],
                                RL[:, t, :].unsqueeze(2).to_broadcast([P, H, D]), ALU.mult) \
                    .then_inc(norm_done, 1)

            def residual(b):
                dve.wait_ge(wo_psum, b + 1)
                v.scalar_tensor_tensor(out=X1[:, b * L:(b + 1) * L], in0=POUT[:, L:2 * L],
                                       scalar=VEC[:, V_BO:V_BO + 1], in1=X[:, b * L:(b + 1) * L],
                                       op0=ALU.add, op1=ALU.add).then_inc(x1_ready, 1)

            def decode():
                dve.wait_ge(dec_psum, 1)
                v.tensor_tensor(UDEC[:, :, 0:K], PST[0][:, 0:K * B].rearrange("p (k b) -> p b k", b=B),
                                BDEC[:, :].unsqueeze(1).to_broadcast([P, B, K]), ALU.add).then_inc(dec_sb, 1)
                v.tensor_scalar(UDECL[:, :], PST[0][0:K, K * B:K * B + B], BDECL[:, 0:1], None, ALU.add) \
                    .then_inc(dec_sb, 1)
                dve.wait_ge(dec_psum, 2)
                v.tensor_copy(ALPHA[:, :], PST[1][:, 0:NF + 1]).then_inc(dec_sb, 1)

            def decode_weights():
                dve.wait_ge(dec_psum, 3)
                v.tensor_copy(UT[:, :, :], PST[2][:, 0:2 * P].rearrange("p (r i) -> p r i", r=2)) \
                    .then_inc(dec_sb, 1)
                dve.wait_ge(dec_psum, 4)
                for j in range(4):
                    v.tensor_copy(WB[:, j:B:4, :], PWB[j][:, 0:2 * P].rearrange("p (r e) -> p r e", r=2)) \
                        .then_inc(dec_sb, 1)
                v.tensor_copy(BB[:, :], PST[0][:, 256:256 + B]).then_inc(dec_sb, 1)

            for s in range(-3, B):
                front, big, now, tail = (0 <= x < B for x in (s + 3, s + 1, s, s - 1))
                for tick in range(12):
                    if tick == 0 and now:
                        split_max(s, 1)
                    if tick == 6 and big:
                        split_max(s + 1, 0)
                    if tick == 3 and front:
                        clip(s + 3)
                    if tick in (5, 7) and tail:
                        normalise(s - 1, (tick - 5) // 2)
                    if tick in (6, 7) and front:
                        rope_sine(s + 3, tick - 6)
                    if tick == 9 and front:
                        rope_sum(s + 3)
                    if tick == 11 and tail:
                        residual(s - 1)
                    if big:
                        reduce_max(s + 1, tick)
                    if tick == 4 and s < 0:
                        set_rows(s + 3)
                if s == -3:
                    decode()
                if s == -2:
                    decode_weights()

            def take_o2(p):
                dve.wait_ge(o2_psum, p + 1)
                wait(dve, h_psum, NF * (p - 1))
                for i in range(2):
                    b = 2 * p + i
                    v.tensor_scalar(O2[:, p % 2, i * L:(i + 1) * L], PIN[:, i * L:(i + 1) * L],
                                    BB[:, b:b + 1], None, ALU.add).then_inc(o2_sb, 1)

            def finish(p):
                dve.wait_ge(f_psum, p + 1)
                v.tensor_scalar(FT[:, p % 2, :], PF[p % 2][:, :], ALPHA[:, NF:NF + 1],
                                VEC[:, V_B2:V_B2 + 1], ALU.mult, ALU.add).then_inc(f_scaled, 1)
                dve.wait_ge(f_scaled, p + 1)
                wait(dve, out_stored[p % 2], 16 * (p // 2))
                v.tensor_tensor(OUT[:, p % 2, :], FT[:, p % 2, :], X1[:, 2 * L * p:2 * L * (p + 1)],
                                ALU.add).then_inc(out_ready, 1)

            take_o2(0)
            normalise(B - 1, 0)
            take_o2(1)
            normalise(B - 1, 1)
            finish(0)
            take_o2(2)
            residual(B - 1)
            finish(1)
            take_o2(3)
            finish(2)
            finish(3)


def kernel(**inputs):
    import numpy as np
    import concourse.bacc as bacc
    from concourse.bass_utils import run_bass_kernel_spmd as run

    a = {k: np.asarray(v) for k, v in inputs.items()}
    bf = np.dtype("bfloat16")

    order = np.arange(C).reshape(H, D).T.reshape(-1)
    wq, wk = a["L0_attn_Wq"][order], a["L0_attn_Wk"][order]

    theta = np.float32(1250) ** (np.float32(-2.0) * np.arange(D // 2, dtype=np.float32) / np.float32(D))
    theta = np.concatenate([theta, theta]).astype(np.float32)
    angle = np.arange(1, L + 1, dtype=np.float32)[None, :] * np.repeat(theta, H)[:, None]
    sign = np.where(np.arange(C) < C // 2, 1.0, -1.0).astype(np.float32)[:, None]
    rope = np.stack([np.cos(angle), sign * np.sin(angle)], axis=1).astype(np.float32)
    rowsq, rowsk = np.zeros((P, P)), np.zeros((P, P))
    rowsk[MROW:MROW + 2] = 1.0
    i = np.arange(P)
    for r in range(32):
        rowsq[MASK0 + r] = np.where(i // 4 == r, 2.0 ** (-42.0 * (i % 4)), 0.0)
        rowsk[MASK0 + r] = np.where(i // 4 == r, -(2.0 ** (-12 + 42.0 * (i % 4))), 0.0)
    for r in range(1, 32):
        rowsq[MASK0 + 31 + r] = i // 4 < r
        rowsk[MASK0 + 31 + r] = np.where(i // 4 == r, -(2.0 ** 60), 0.0)

    col = lambda v: v.reshape(-1, P).T
    vecs = np.concatenate([col(a["L0_cond_bias"]), col(a["L0_cond_affine_b"]), col(a["L0_attn_bq"][order]),
                           col(a["L0_attn_bk"][order]), col(a["L0_attn_bv"]), col(a["L0_attn_bo"]),
                           col(a["L0_ffn_b2"]), col(a["L0_ffn_b1"])], axis=1)
    bdec = a["L0_cond2_b_dec"].reshape(C + 1, K)
    arrays = {
        "xT": a["x"].reshape(B * L, C).T,
        "condT": a["cond_512"].T,
        "affT": a["L0_cond_affine_w"].T,
        "wT": a["L0_cond_weight"].T,
        "wqkvT": np.concatenate([wq, wk, a["L0_attn_Wv"]], axis=0).T,
        "woT": a["L0_attn_Wo"].T,
        "vecs": vecs,
        "wdecT": a["L0_cond2_W_dec"].reshape(W, C + 1, K).transpose(0, 2, 1),
        "bdec": bdec[:C],
        "bdecl": bdec[C:].T,
        "vmat": a["L0_cond2_V"],
        "w1T": a["L0_ffn_w1"].T,
        "w2T": a["L0_ffn_w2"].T.reshape(NF, P, C).transpose(1, 0, 2),
        "rope": rope,
        "rowsq": rowsq.astype(bf),
        "rowsk": rowsk.astype(bf),
        "zeros2": np.zeros((2, H, L), bf),
        "ident": np.eye(P, dtype=np.float32),
        "identb": np.eye(P).astype(bf),
    }
    arrays = {k: np.ascontiguousarray(v) for k, v in arrays.items()}
    nc = bacc.Bacc("TRN2", target_bir_lowering=False, num_devices=1)
    args = [nc.dram_tensor(k, v.shape, mybir.dt.from_np(v.dtype), kind="ExternalInput").ap()
            for k, v in arrays.items()]
    out = nc.dram_tensor("outT", (C, B * L), F32, kind="ExternalOutput").ap()
    build(nc, *args, out)
    r = run(nc, [arrays], core_ids=[0])
    return r.results[0]["outT"].T.reshape(B, L, C)
```

```python
from contextlib import ExitStack

import concourse.bass as bass
from concourse import mybir

ALU = mybir.AluOpType
ACT = mybir.ActivationFunctionType
AX = mybir.AxisListType
F32 = mybir.dt.float32
BF16 = mybir.dt.bfloat16

P = 128
B = 8
L = 256
T = L // P
C = 128
H = 16
D = C // H
W = 64
K = 30
F = 512
NF = F // P

SLOTS = 3
STACK = 6 * D
MROW = STACK
KST = 65
UC = K // 2 * (C + 1)
MASK0 = 65

V_BIAS, V_AFFB, V_BQ, V_BK, V_BV, V_BO, V_B2, V_B1 = 0, 1, 2, 3, 4, 5, 6, 7
NV = V_B1 + NF


def build(nc, xT, condaff, wvecs, wqkvT, rope, rowsb, wdec, mats, vdec, w12, w12n, zeros2, outT):
    with ExitStack() as ctx:
        def sb(name, shape, dt=F32):
            return ctx.enter_context(nc.sbuf_tensor(name, shape, dt))

        def sem(name):
            return ctx.enter_context(nc.semaphore(name))

        X = sb("X", [P, B * L])
        CONDAFF = sb("CONDAFF", [2 * W, 2 * B + C])
        COND, AFF = CONDAFF[0:W, 0:B], CONDAFF[0:W, 2 * B:]
        COND2 = CONDAFF[:, 0:2 * B]
        WVEC = sb("WVEC", [P, NV + C])
        VEC, WM = WVEC[:, 0:NV], WVEC[:, NV:]
        WQKV = sb("WQKV", [P, 3 * C])
        ROPE = sb("ROPE", [P, 2, L])
        ROWSB = sb("ROWSB", [P, 3, P], BF16)
        ROWSQ, ROWSK, IDB = (ROWSB[:, i, :] for i in range(3))
        MATS = sb("MATS", [P, 2 * C])
        VDEC = sb("VDEC", [K, C + B * (C + 1)])
        ID, WO = MATS[:, 0:C], MATS[:, C:]
        VMAT, BDEC = VDEC[:, 0:C], VDEC[:, C:].rearrange("k (b i) -> k b i", b=B)
        W12 = sb("W12", [P, 2, F])
        STY = sb("STY", [P, B])
        STY2 = sb("STY2", [P, B])
        WM2 = sb("WM2", [P, C])
        DEM = sb("DEM", [P, 2, B])
        DCO = sb("DCO", [P, B])
        UDEC = sb("UDEC", [2 * B, UC])
        UT = sb("UT", [K, B, C + 1])
        WB = sb("WB", [P, B, C])
        BB = sb("BB", [P, B])
        SG1 = sb("SG1", [P, F], BF16)
        SG2 = sb("SG2", [P, F], BF16)
        SG2F = sb("SG2F", [P, F])
        O2P = sb("O2P", [P, 2, 3, 2 * L], BF16)
        ALPHA = sb("ALPHA", [P, NF + 1])
        XM = sb("XM", [P, 2, L])
        Y1 = sb("Y1", [P, L])
        Y = sb("Y", [P, 2, L])
        QK = sb("QK", [P, 2, L])
        RC = sb("RC", [P, 2, L])
        RS = sb("RS", [P, 2, L])
        RP = sb("RP", [P, 2, 2, L])
        PARTS = sb("PARTS", [P, 3, 2, L], BF16)
        REST = sb("REST", [P, 2, L])
        QS = [sb(f"QS{i}", [P, H, L], BF16) for i in range(SLOTS)]
        KS = [sb(f"KS{i}", [P, H, L], BF16) for i in range(SLOTS)]
        VA = [sb(f"VA{i}", [P, T, H, 32]) for i in range(4)]
        MX = sb("MX", [P, 2, T, H])
        MP = sb("MP", [P, 2, T, 2, 8], BF16)
        NM = sb("NM", [P, 2, L], BF16)
        PX = sb("PX", [P, 12, 1024])
        WDEC = PX[:, 8:10, :].rearrange("p a c -> p (a c)")[:, 0:UC]
        W12N = PX[:, 10, :].rearrange("p (s f) -> p s f", s=2)
        ABS = PX[:, 11, 0:F]
        HS = PX[:, 3:5, :].rearrange("p m (n t) -> p (m n) t", n=2)
        HP = [PX[:, m:m + 3, :].rearrange("p m t -> p (m t)").bitcast(BF16)
              .rearrange("p (n i t) -> p n i t", n=NF, i=3) for m in (0, 7)]
        O2 = PX[:, 5, :].rearrange("p (s t) -> p s t", s=2)
        OUT = PX[:, 6, :].rearrange("p (s t) -> p s t", s=2)
        OT = sb("OT", [P, 4, L])
        RL = sb("RL", [P, T, H])
        ON = sb("ON", [P, T, C])
        AT = sb("AT", [P, L])
        X1 = sb("X1", [P, B * L])
        FT = sb("FT", [P, 2, 2 * L])

        SCR = [nc.dram_tensor(f"parts{i}", [4, 2, P, L], BF16, kind="Internal").ap() for i in range(2)]

        SCRU = nc.dram_tensor("decoded", [2 * B, UC], F32, kind="Internal").ap()

        PST = [ctx.enter_context(nc.psum_tensor(f"PST{i}", [P, 512], F32)) for i in range(3)]
        PSM = [ctx.enter_context(nc.psum_tensor(f"PSM{i}", [P, 512], F32)) for i in range(3)]
        POUT = ctx.enter_context(nc.psum_tensor("POUT", [P, 512], F32))
        PIN = ctx.enter_context(nc.psum_tensor("PIN", [P, 512], F32))
        PH = [PSM[0], PST[0], PST[1], PST[2]]
        PF = [PSM[1], PSM[2]]
        PWB = [PSM[0], PSM[1], PSM[2]]
        PDEC = [PST[0], PST[1], PST[2], POUT]

        in_first = sem("in_first")
        in_x0 = sem("in_x0")
        in_x = sem("in_x")
        in_qkv = sem("in_qkv")
        in_rope = sem("in_rope")
        in_rows = sem("in_rows")
        in_dec = sem("in_dec")
        in_mats = sem("in_mats")
        in_vdec = sem("in_vdec")
        in_ffn = sem("in_ffn")
        prep = sem("prep")
        prep_psum = sem("prep_psum")
        prep_act = sem("prep_act")
        rows_copied = sem("rows_copied")
        rows_set = sem("rows_set")
        va_set = sem("va_set")
        xm_ready = sem("xm_ready")
        y_psum = sem("y_psum")
        y1_ready = sem("y1_ready")
        y_ready = sem("y_ready")
        qk_psum = sem("qk_psum")
        qk_sb = sem("qk_sb")
        v_psum = sem("v_psum")
        v_ready = sem("v_ready")
        rope_terms = sem("rope_terms")
        rope_cos = sem("rope_cos")
        rope_ready = sem("rope_ready")
        part1_made = sem("part1_made")
        part_made = sem("part_made")
        scratch = [sem(f"scratch{i}") for i in range(2)]
        stack = [sem(f"stack{i}") for i in range(SLOTS)]
        m_rows = [[sem(f"m_rows{i}{j}") for j in range(2)] for i in range(SLOTS)]
        smax_psum = sem("smax_psum")
        smax_read = sem("smax_read")
        m_hi = sem("m_hi")
        m_parts = sem("m_parts")
        m_psum = sem("m_psum")
        m_sb = sem("m_sb")
        st_psum = sem("st_psum")
        exp_done = sem("exp_done")
        mask_done = sem("mask_done")
        o_psum = sem("o_psum")
        o_sb = sem("o_sb")
        tr_psum = sem("tr_psum")
        rl_ready = sem("rl_ready")
        norm_done = sem("norm_done")
        at_psum = sem("at_psum")
        at_sb = sem("at_sb")
        wo_psum = sem("wo_psum")
        x1_ready = sem("x1_ready")
        dec_psum = sem("dec_psum")
        dec_sb = sem("dec_sb")
        dec_scratch = sem("dec_scratch")
        dec_turned = sem("dec_turned")
        wb_psum = sem("wb_psum")
        ut_ready = sem("ut_ready")
        wb_ready = sem("wb_ready")
        alpha_ready = sem("alpha_ready")
        sign_ready = sem("sign_ready")
        o2_psum = sem("o2_psum")
        o2_left = sem("o2_left")
        o2_parts = sem("o2_parts")
        h_psum = sem("h_psum")
        h_sb = sem("h_sb")
        h_rest = sem("h_rest")
        h_second = sem("h_second")
        h_third = sem("h_third")
        h_split = sem("h_split")
        f_psum = sem("f_psum")
        f_scaled = sem("f_scaled")
        out_ready = sem("out_ready")
        out_stored = [sem(f"out_stored{i}") for i in range(2)]

        def wait(eng, s, n):
            if n > 0:
                eng.wait_ge(s, n)

        LAST = B // 2 - 1
        N_DEC = -(-UC // 512)
        N_WB = 3
        STACKED = 4

        def stack_value(b):
            n = 0
            for bb in range(b % SLOTS, b + 1, SLOTS):
                n += 16 * (STACKED + (bb >= SLOTS))
            return n

        def unit_of(n):
            half, u = divmod(n, 6)
            return (half, 8 * half + 4 * u, 4, 0) if u < 2 else (half, 8 * half + 2 * (u - 2), 2, 1)

        block = ctx.enter_context(nc.Block())

        @block.sync
        def _(sp):
            sp.dma_start(CONDAFF[:, :], condaff).then_inc(in_first, 16)
            sp.dma_start(WVEC[:, :], wvecs).then_inc(in_first, 16)
            sp.dma_start(X[:, 0:2 * L], xT[:, 0:2 * L]).then_inc(in_x0, 16)
            sp.dma_start(WQKV[:, :], wqkvT).then_inc(in_qkv, 16)
            sp.dma_start(ROWSB[:, :, :], rowsb).then_inc(in_rows, 16)
            sp.dma_start(ROPE[:, :, :], rope).then_inc(in_rope, 16)
            sp.dma_start(WDEC[:, :], wdec).then_inc(in_dec, 16)
            sp.dma_start(X[:, 2 * L:], xT[:, 2 * L:]).then_inc(in_x, 16)
            sp.dma_start(MATS[:, :], mats).then_inc(in_mats, 16)
            sp.dma_start(VDEC[:, :], vdec).then_inc(in_vdec, 16)
            sp.dma_start(W12[:, :, :], w12).then_inc(in_ffn, 16)
            sp.dma_start(W12N[:, :, :], w12n).then_inc(in_ffn, 16)

            sp.wait_ge(rows_set, 2)
            for S in (QS, KS):
                sp.dma_start(S[2][MROW:, :, :], S[0][MROW:, :, :]).then_inc(rows_copied, 16)

            def store_parts(b):
                sp.wait_ge(part1_made, b + 1)
                if b >= 2:
                    sp.wait_ge(stack[(b - 2) % SLOTS], stack_value(b - 2))
                for first in (0, 3):
                    sp.dma_start(SCR[b % 2][first].rearrange("s p t -> p s t"), PARTS[:, 0, :, :]) \
                        .then_inc(scratch[b % 2], 16)
                sp.wait_ge(part_made, 3 * (b + 1))
                sp.dma_start(SCR[b % 2][1:3].rearrange("n s p t -> p (n s) t"),
                             PARTS[:, 1:3, :, :].rearrange("p n s t -> p (n s) t")) \
                    .then_inc(scratch[b % 2], 16)

            def stack_rows(b):
                s = b % SLOTS
                sp.wait_ge(scratch[b % 2], 48 * (b // 2 + 1))
                if s < 2:
                    sp.wait_ge(rows_set, 2 * (s + 1))
                else:
                    sp.wait_ge(rows_copied, 32)
                if b >= SLOTS:
                    sp.wait_ge(st_psum, 12 * (b - SLOTS + 1))
                    sp.dma_start(QS[s][MROW:MROW + 2, :, :], zeros2).then_inc(stack[s], 16)
                q, k = (SCR[b % 2][:, i].rearrange("n (d h) t -> n d (h t)", d=D) for i in range(2))
                sp.dma_start(QS[s][0:16, :, :].rearrange("p h t -> p (h t)"), q[0:2]).then_inc(stack[s], 16)
                sp.dma_start(KS[s][0:32, :, :].rearrange("p h t -> p (h t)"), k[0:4]).then_inc(stack[s], 16)
                sp.dma_start(QS[s][16:48, :, :].rearrange("p h t -> p (h t)"), q[0:4]).then_inc(stack[s], 16)
                sp.dma_start(KS[s][32:48, :, :].rearrange("p h t -> p (h t)"), k[0:2]).then_inc(stack[s], 16)

            def place_max(b, half):
                s = b % SLOTS
                sp.wait_ge(m_sb, 2 * b + half + 1)
                sp.wait_ge(rows_copied, 32)
                for part in range(2):
                    sp.dma_start(QS[s][MROW + part:MROW + part + 1, 8 * half:8 * half + 8, :],
                                 NM[8 * part:8 * part + 8, half, :]).then_inc(m_rows[s][half], 16)

            def turn_decoded():
                sp.wait_ge(dec_sb, N_DEC)
                sp.dma_start(SCRU, UDEC[:, :]).then_inc(dec_scratch, 16)
                sp.wait_ge(dec_scratch, 16)
                for a in range(2):
                    sp.dma_start(UT[K // 2 * a:K // 2 * (a + 1), :, :],
                                 SCRU[B * a:B * (a + 1)].rearrange("b (k i) -> k b i", k=K // 2)) \
                        .then_inc(dec_turned, 16)

            for s in range(-3, B + 1):
                if 0 <= s < B:
                    place_max(s, 1)
                if 0 <= s + 2 < B:
                    stack_rows(s + 2)
                if 0 <= s + 1 < B:
                    place_max(s + 1, 0)
                if 0 <= s + 3 < B:
                    store_parts(s + 3)
                if s == B - 4:
                    turn_decoded()
            for p in range(LAST):
                sp.wait_ge(out_ready, p + 1)
                sp.dma_start(outT[:, 2 * L * p:2 * L * (p + 1)], OUT[:, p % 2, :]).then_inc(out_stored[p % 2], 16)
            for i in range(2):
                sp.wait_ge(out_ready, LAST + 1 + i)
                at = (2 * LAST + i) * L
                sp.dma_start(outT[:, at:at + L], OUT[:, LAST % 2, i * L:(i + 1) * L]) \
                    .then_inc(out_stored[LAST % 2], 16)
            sp.wait_ge(out_stored[0], 16 * 2)
            sp.wait_ge(out_stored[1], 16 * 3)

        @block.tensor
        def _(pe):
            mm = pe.matmul

            pe.wait_ge(in_first, 32)
            mm(PIN[:, 0:B], AFF[:, :], COND[:, :], start=True, stop=True).then_inc(prep_psum, 1)
            pe.wait_ge(prep, 3)
            mm(PSM[0][:, 0:B], WM2[:, :], STY2[:, :], start=True, stop=True).then_inc(prep_psum, 1)

            def y_product(b):
                pe.wait_ge(xm_ready, b + 1)
                if b == 0:
                    pe.wait_ge(prep, 1)
                else:
                    pe.wait_ge(v_ready, b)
                if b >= SLOTS:
                    pe.wait_ge(m_sb, 2 * (b - SLOTS) + 2)
                mm(PIN[:, 0:L], WM[:, :], XM[:, b % 2, :], start=True, stop=True).then_inc(y_psum, 1)

            def qk_product(b):
                if b == 0:
                    pe.wait_ge(in_qkv, 16)
                pe.wait_ge(y_ready, b + 1)
                if b >= SLOTS:
                    pe.wait_ge(m_sb, 2 * (b - SLOTS) + 2)
                mm(PIN[:, 0:L], WQKV[:, 0:C], Y[:, b % 2, :], start=True, stop=True)
                mm(PIN[:, L:2 * L], WQKV[:, C:2 * C], Y[:, b % 2, :], start=True, stop=True) \
                    .then_inc(qk_psum, 1)

            def v_product(b):
                pe.wait_ge(qk_sb, 2 * (b + 1))
                if b >= SLOTS:
                    pe.wait_ge(m_sb, 2 * (b - SLOTS) + 3)
                for t in range(T):
                    m = mm(PIN[:, t * P:(t + 1) * P], Y[:, b % 2, t * P:(t + 1) * P], WQKV[:, 2 * C:],
                           start=True, stop=True)
                m.then_inc(v_psum, 1)

            def scores_for_max(b, n):
                s = b % SLOTS
                _, h0, nh, t = unit_of(n)
                if n == 0:
                    pe.wait_ge(stack[s], stack_value(b))
                    pe.wait_ge(prep, 4)
                wait(pe, smax_read, 12 * b + n - 2)
                out = PSM[(12 * b + n) % 3]
                for i in range(nh):
                    h = h0 + i
                    q = slice(t * P, (t + 1) * P)
                    at = i * (t + 1) * P
                    if t:
                        mm(out[:, at:at + P], QS[s][0:KST, h, q], KS[s][0:KST, h, 0:P], start=True, stop=True)
                        at += P
                    m = mm(out[:, at:at + P], QS[s][:, h, q], KS[s][:, h, q], start=True, stop=True)
                m.then_inc(smax_psum, 1)

            def turn_max(b, half):
                pe.wait_ge(m_parts, 2 * b + half + 1)
                wait(pe, m_sb, 2 * b + half)
                if b == 0 and half == 0:
                    pe.wait_ge(in_rows, 16)
                    pe.wait_ge(v_ready, SLOTS)
                elif half == 0:
                    pe.wait_ge(qk_sb, 2 * min(b + 3, B))
                else:
                    pe.wait_ge(v_ready, min(b + 3, B))
                for t in range(T):
                    m = pe.transpose(PIN[0:16, 384 + 64 * t:448 + 64 * t].bitcast(BF16),
                                     MP[:, half, t, :, :].rearrange("p a h -> p (a h)"),
                                     IDB[:, :])
                m.then_inc(m_psum, 1)

            def scores(b, u):
                s = b % SLOTS
                half, w = divmod(u, 6)
                if w == 0:
                    pe.wait_ge(m_rows[s][half], 32 * (b // SLOTS + 1))
                if b == 0 and u == 0:
                    pe.wait_ge(dec_sb, N_DEC)
                wait(pe, exp_done, 12 * b + u - 2)
                out = PST[(12 * b + u) % 3]
                if w < 4:
                    for i in range(2):
                        h = 8 * half + 2 * w + i
                        m = mm(out[:, i * L:(i + 1) * L], KS[s][0:KST, h, 0:P], QS[s][0:KST, h, :],
                               start=True, stop=True)
                else:
                    for i in range(4):
                        h = 8 * half + 4 * (w - 4) + i
                        m = mm(out[:, i * P:(i + 1) * P], KS[s][0:KST, h, P:L], QS[s][0:KST, h, P:L],
                               start=True, stop=True)
                m.then_inc(st_psum, 1)

            def pv(b, half, g):
                if g == 0:
                    if half == 0:
                        wait(pe, x1_ready, b)
                        pe.wait_ge(v_ready, b + 1)
                    else:
                        pe.wait_ge(o_sb, 2 * b + 1)
                    pe.wait_ge(mask_done, 6 * b + 3 * half + 3)
                px = 6 * (b % 2) + 3 * half
                for j in range(4):
                    h = 8 * half + 4 * g + j
                    mm(POUT[32 * j:32 * j + 32, g * L:(g + 1) * L], VA[b % 4][:, 0, h, :],
                       PX[:, px + g, j * L:(j + 1) * L], start=True, stop=False, skip_group_check=True)
                for j in range(4):
                    h = 8 * half + 4 * g + j
                    m = mm(POUT[32 * j:32 * j + 32, g * L + P:(g + 1) * L], VA[b % 4][:, 1, h, :],
                           PX[:, px + 2, (4 * g + j) * P:(4 * g + j + 1) * P], start=False, stop=True,
                           skip_group_check=True)
                if g == 1:
                    m.then_inc(o_psum, 1)

            def turn_out(b, t):
                pe.wait_ge(o_sb, 2 * b + 2)
                if t:
                    pe.wait_ge(norm_done, 2 * b + 1)
                for g in range(4):
                    m = pe.transpose(POUT[:, g * P:(g + 1) * P], OT[:, g, t * P:(t + 1) * P], ID[:, :])
                m.then_inc(tr_psum, 1)

            def turn_heads(b):
                pe.wait_ge(norm_done, 2 * b + 2)
                for t in range(T):
                    m = pe.transpose(POUT[:, t * P:(t + 1) * P], ON[:, t, :], ID[:, :])
                m.then_inc(at_psum, 1)

            def out_product(b):
                pe.wait_ge(at_sb, b + 1)
                mm(POUT[:, L:2 * L], WO[:, :], AT[:, :], start=True, stop=True).then_inc(wo_psum, 1)

            def decode(n):
                if n == 0:
                    pe.wait_ge(in_dec, 16)
                cols = slice(512 * n, min(512 * (n + 1), UC))
                mm(PDEC[n][0:2 * B, 0:cols.stop - cols.start], COND2, WDEC[:, cols], start=True, stop=True) \
                    .then_inc(dec_psum, 1)

            def decode_weights():
                pe.wait_ge(in_vdec, 16)
                pe.wait_ge(ut_ready, 1)
                pe.wait_ge(smax_read, 12 * B)
                for b in range(B):
                    mm(PWB[b // 4][:, b % 4 * P:(b % 4 + 1) * P], UT[:, b, 0:C], VMAT, start=True, stop=True)
                mm(PWB[2][:, 0:B], VMAT, UT[:, :, C], start=True, stop=True).then_inc(wb_psum, 1)

            y_product(0)
            qk_product(0)
            decode(0)
            v_product(0)
            y_product(1)
            decode(1)
            qk_product(1)
            v_product(1)
            y_product(2)
            qk_product(2)
            scores_for_max(0, 0)
            v_product(2)
            scores_for_max(0, 1)
            decode(2)
            for n in range(2, 8):
                scores_for_max(0, n)
            decode(3)
            turn_max(0, 0)
            for n in range(8, 12):
                scores_for_max(0, n)
            for s in range(B - 1):
                front, tail = s + 3 < B, s > 0
                for tick in range(12):
                    if tick == 6 and tail:
                        turn_out(s - 1, 1)
                    if tick == 7:
                        turn_max(s + 1, 0)
                    if tick == 8 and tail:
                        turn_heads(s - 1)
                    if tick == 10 and tail:
                        out_product(s - 1)
                    if tick == 10 and front:
                        v_product(s + 3)
                    scores_for_max(s + 1, tick)
                    if tick == 1:
                        turn_max(s, 1)
                    if tick == 3 and front:
                        y_product(s + 3)
                    if tick == 3 and tail:
                        pv(s - 1, 1, 0)
                        pv(s - 1, 1, 1)
                    if tick == 5 and tail:
                        turn_out(s - 1, 0)
                    if tick == 5 and front:
                        qk_product(s + 3)
                    scores(s, tick)
                pv(s, 0, 0)
                pv(s, 0, 1)

            def o2_product(p):
                if p == 0:
                    pe.wait_ge(wb_ready, N_WB)
                    pe.wait_ge(m_sb, 2 * B)
                else:
                    pe.wait_ge(o2_parts, 5 * (p - 1) + 2)
                pe.wait_ge(x1_ready, 2 * p + 2)
                for i in range(2):
                    b = 2 * p + i
                    m = mm(PIN[:, i * L:(i + 1) * L], WB[:, b, :], X1[:, b * L:(b + 1) * L],
                           start=True, stop=True)
                m.then_inc(o2_psum, 1)

            def h_product(p, n):
                if p == 0 and n == 0:
                    pe.wait_ge(sign_ready, 3)
                    pe.wait_ge(wb_ready, N_WB)
                if p == 0 and n == 1:
                    pe.wait_ge(exp_done, 12 * B)
                pe.wait_ge(o2_parts, 5 * (p + 1))
                wait(pe, h_sb, 2 * (NF * (p - 1) + n + 1) if p else 0)
                for i in range(3):
                    m = mm(PH[n][:, :], SG1[:, n * P:(n + 1) * P], O2P[:, p % 2, i, :], start=(i == 0),
                           stop=(i == 2))
                m.then_inc(h_psum, 1)

            def last_f_products():
                pe.wait_ge(h_sb, 2 * NF * LAST + NF)
                for i in range(2):
                    pe.wait_ge(f_scaled, LAST - 1 + i)
                    for n in range(NF):
                        m = mm(PF[(LAST + i) % 2][:, 0:L], SG2F[:, n * P:(n + 1) * P],
                               HS[:, n, i * L:(i + 1) * L], start=(n == 0), stop=(n == NF - 1))
                    m.then_inc(f_psum, 1)

            def f_product(p, n):
                if n == 0:
                    wait(pe, f_scaled, p - 1)
                if n % 2 == 0:
                    pe.wait_ge(h_third, 2 * p + n // 2 + 1)
                else:
                    pe.wait_ge(h_split, 3 * (2 * p + n // 2 + 1))
                for i in range(3):
                    m = mm(PF[p % 2][:, :], SG2[:, n * P:(n + 1) * P], HP[p % 2][:, n, i, :],
                           start=(n == 0 and i == 0), stop=(n == NF - 1 and i == 2))
                if n == NF - 1:
                    m.then_inc(f_psum, 1)

            scores(B - 1, 0)
            decode_weights()
            pv(B - 2, 1, 0)
            turn_max(B - 1, 1)
            scores(B - 1, 1)
            pv(B - 2, 1, 1)
            scores(B - 1, 2)
            o2_product(0)
            turn_out(B - 2, 0)
            for n in range(3, 6):
                scores(B - 1, n)
            turn_out(B - 2, 1)
            scores(B - 1, 6)
            scores(B - 1, 7)
            turn_heads(B - 2)
            scores(B - 1, 8)
            scores(B - 1, 9)
            out_product(B - 2)
            scores(B - 1, 10)
            o2_product(1)
            pv(B - 1, 0, 0)
            scores(B - 1, 11)
            pv(B - 1, 0, 1)
            h_product(0, 0)
            h_product(0, 1)
            o2_product(2)
            pv(B - 1, 1, 0)
            h_product(0, 2)
            h_product(0, 3)
            h_product(1, 0)
            pv(B - 1, 1, 1)
            turn_out(B - 1, 0)
            h_product(1, 1)
            h_product(1, 2)
            f_product(0, 0)
            turn_out(B - 1, 1)
            turn_heads(B - 1)
            f_product(0, 1)
            h_product(1, 3)
            out_product(B - 1)
            f_product(0, 2)
            f_product(0, 3)
            h_product(2, 0)
            o2_product(3)
            for n in range(1, 4):
                h_product(2, n)
            for n in range(4):
                f_product(1, n)
            for n in range(4):
                h_product(3, n)
            for n in range(4):
                f_product(2, n)
            last_f_products()

        @block.scalar
        def _(act):
            def modulate(b):
                if b == 0:
                    act.wait_ge(in_x0, 16)
                    act.wait_ge(prep, 1)
                if b == 2:
                    act.wait_ge(in_x, 16)
                wait(act, y_psum, b - 1)
                nc.scalar.activation(XM[:, b % 2, :], X[:, b * L:(b + 1) * L], ACT.Copy,
                                     scale=STY[:, b:b + 1]).then_inc(xm_ready, 1)

            def demodulate(b):
                if b == 0:
                    act.wait_ge(prep, 5)
                act.wait_ge(y_psum, b + 1)
                wait(act, y_ready, b)
                nc.scalar.activation(Y1[:, :], PIN[:, 0:L], ACT.Identity, scale=DCO[:, b:b + 1],
                                     bias=VEC[:, V_BIAS:V_BIAS + 1]).then_inc(y1_ready, 1)

            def take_qk(b):
                act.wait_ge(qk_psum, b + 1)
                wait(act, rope_terms, 2 * b)
                wait(act, rope_cos, b)
                for i, v in ((0, V_BQ), (1, V_BK)):
                    nc.scalar.activation(QK[:, i, :], PIN[:, i * L:(i + 1) * L], ACT.Identity,
                                         bias=VEC[:, v:v + 1]).then_inc(qk_sb, 1)

            def part1(b):
                act.wait_ge(rope_ready, b + 1)
                if b:
                    act.wait_ge(scratch[(b - 1) % 2], 48 * ((b - 1) // 2 + 1))
                nc.scalar.activation(PARTS[:, 0, :, :], RP[:, b % 2, :, :], ACT.Copy).then_inc(part1_made, 1)

            def take_v(b):
                if b == 0:
                    act.wait_ge(va_set, 8)
                act.wait_ge(v_psum, b + 1)
                wait(act, o_psum, 2 * (b - 4) + 2)
                nc.scalar.activation(VA[b % 4][:, :, :, 0:D],
                                     PIN[:, 0:L].rearrange("p (t h d) -> p t h d", t=T, d=D),
                                     ACT.Copy).then_inc(v_ready, 1)

            def exponent(b, u):
                act.wait_ge(st_psum, 12 * b + u + 1)
                if b >= 2:
                    act.wait_ge(o_psum, 2 * (b - 2) + u // 6 + 1)
                nc.scalar.activation(PX[:, 6 * (b % 2) + u // 2, 512 * (u % 2):512 * (u % 2) + 512],
                                     PST[(12 * b + u) % 3][:, :], ACT.Exp, scale=float(D) ** -0.5) \
                    .then_inc(exp_done, 1)

            def take_out(b, half):
                act.wait_ge(o_psum, 2 * b + half + 1)
                wait(act, tr_psum, 2 * b)
                nc.scalar.activation(OT[:, 2 * half:2 * half + 2, :].rearrange("p g t -> p (g t)"),
                                     POUT[:, :], ACT.Copy).then_inc(o_sb, 1)

            def take_heads(b):
                act.wait_ge(at_psum, b + 1)
                wait(act, wo_psum, b)
                nc.scalar.activation(AT[:, :], POUT[:, 0:L], ACT.Identity,
                                     bias=VEC[:, V_BV:V_BV + 1]).then_inc(at_sb, 1)

            def take_decoded(n):
                act.wait_ge(dec_psum, n + 1)
                cols = slice(512 * n, min(512 * (n + 1), UC))
                nc.scalar.activation(UDEC[:, cols], PDEC[n][0:2 * B, 0:cols.stop - cols.start], ACT.Copy) \
                    .then_inc(dec_sb, 1)

            def take_max(b, half):
                act.wait_ge(m_psum, 2 * b + half + 1)
                if b:
                    act.wait_ge(m_rows[(b - 1) % SLOTS][half], 32 * ((b - 1) // SLOTS + 1))
                nc.scalar.activation(NM[0:16, half, :], PIN[0:16, 384:512].bitcast(BF16), ACT.Copy) \
                    .then_inc(m_sb, 1)

            def signs():
                act.wait_ge(in_ffn, 32)
                nc.scalar.activation(SG1[:, :], W12[:, 0, :], ACT.Sign).then_inc(sign_ready, 1)
                nc.scalar.activation(SG2[:, :], W12[:, 1, :], ACT.Sign).then_inc(sign_ready, 1)
                nc.scalar.activation(SG2F[:, :], W12[:, 1, :], ACT.Sign).then_inc(sign_ready, 1)

            def mean_magnitudes():
                act.wait_ge(in_ffn, 32)
                for n in range(NF):
                    nc.scalar.activation(ABS[:, n * P:(n + 1) * P], W12N[:, 0, n * P:(n + 1) * P], ACT.Abs,
                                         scale=1.0 / C, accum_out=ALPHA[:, n:n + 1]).then_inc(alpha_ready, 1)
                act.wait_ge(alpha_ready, NF)
                nc.scalar.activation(ABS[:, :], W12N[:, 1, :], ACT.Abs, scale=1.0 / F,
                                     accum_out=ALPHA[:, NF:NF + 1]).then_inc(alpha_ready, 1)

            def demodulation_root():
                act.wait_ge(prep, 4)
                nc.scalar.activation(DEM[:, 1, :], DEM[:, 0, :], ACT.Sqrt).then_inc(prep_act, 1)

            modulate(0)
            demodulation_root()
            modulate(1)
            demodulate(0)
            take_qk(0)
            take_v(0)
            modulate(2)
            part1(0)
            demodulate(1)
            take_qk(1)
            take_v(1)
            modulate(3)
            part1(1)
            demodulate(2)
            take_decoded(0)
            take_qk(2)
            take_v(2)
            take_decoded(1)
            take_decoded(2)
            signs()
            part1(2)
            mean_magnitudes()
            take_max(0, 0)
            take_decoded(3)
            for s in range(B - 1):
                front, tail = s + 3 < B, s > 0
                for tick in range(12):
                    if tick == 0 and tail:
                        take_out(s - 1, 0)
                    if tick == 1:
                        take_max(s, 1)
                    if tick == 2 and front:
                        demodulate(s + 3)
                    if tick == 2 and tail:
                        take_out(s - 1, 1)
                    if tick == 4 and s + 4 < B:
                        modulate(s + 4)
                    if tick == 4 and front:
                        take_qk(s + 3)
                    if tick == 7 and tail:
                        take_heads(s - 1)
                    if tick == 7:
                        take_max(s + 1, 0)
                    if tick == 8 and front:
                        part1(s + 3)
                    if tick == 10 and front:
                        take_v(s + 3)
                    exponent(s, tick)

            def hidden(p, n):
                if p == 0 and n == 0:
                    act.wait_ge(alpha_ready, NF + 1)
                    act.wait_ge(o_psum, 2 * (B - 1))
                act.wait_ge(h_psum, NF * p + n + 1)
                wait(act, f_psum, p - 1)
                if p and n % 2 == 0:
                    act.wait_ge(h_third, 2 * (p - 1) + n // 2 + 1)
                elif p:
                    act.wait_ge(h_split, 3 * (2 * (p - 1) + n // 2 + 1))
                if p == 1 and n == 0:
                    act.wait_ge(o_psum, 2 * B)
                for dst in (HS[:, n, :], HP[p % 2][:, n, 0, :])[:1 if p == LAST else 2]:
                    nc.scalar.activation(dst, PH[n][:, :], ACT.Gelu, scale=ALPHA[:, n:n + 1],
                                         bias=VEC[:, V_B1 + n:V_B1 + n + 1]).then_inc(h_sb, 1)

            def second_part(p, n):
                act.wait_ge(h_rest, 2 * p + n // 2 + 1)
                nc.scalar.activation(HP[p % 2][:, n, 1, :], HS[:, n, :], ACT.Copy).then_inc(h_second, 1)

            exponent(B - 1, 0)
            take_out(B - 2, 0)
            take_max(B - 1, 1)
            take_out(B - 2, 1)
            for n in range(1, 7):
                exponent(B - 1, n)
            take_heads(B - 2)
            for n in range(7, 12):
                exponent(B - 1, n)
            take_out(B - 1, 0)
            for n in range(3):
                hidden(0, n)
            take_out(B - 1, 1)
            second_part(0, 0)
            hidden(0, 3)
            hidden(1, 0)
            second_part(0, 2)
            hidden(1, 1)
            take_heads(B - 1)
            hidden(1, 2)
            second_part(1, 0)
            hidden(1, 3)
            second_part(1, 2)
            for n in range(4):
                hidden(2, n)
            second_part(2, 0)
            second_part(2, 2)
            for n in range(4):
                hidden(3, n)

        @block.gpsimd
        def _(pool):
            for i in range(4):
                pool.memset(VA[i][:, :, :, D:32], 0.0).then_inc(va_set, 1)
            pool.wait_ge(va_set, 4)
            for i in range(4):
                pool.memset(VA[i][:, :, :, D:D + 1], 1.0).then_inc(va_set, 1)

            def cosine(b):
                if b == 0:
                    pool.wait_ge(in_rope, 16)
                pool.wait_ge(qk_sb, 2 * b + 2)
                wait(pool, rope_ready, b)
                pool.tensor_tensor(RC[:, :, :], QK[:, :, :], ROPE[:, 0, :].unsqueeze(1).to_broadcast([P, 2, L]),
                                   ALU.mult).then_inc(rope_cos, 1)

            def split(b):
                pool.wait_ge(part1_made, b + 1)
                pool.tensor_tensor(REST[:, :, :], RP[:, b % 2, :, :], PARTS[:, 0, :, :], ALU.subtract) \
                    .then_inc(part_made, 1)
                pool.wait_ge(part_made, 3 * b + 1)
                pool.tensor_scalar(PARTS[:, 1, :, :], REST[:, :, :], 1.0, 1.0, ALU.mult, ALU.mult) \
                    .then_inc(part_made, 1)
                pool.wait_ge(part_made, 3 * b + 2)
                pool.tensor_tensor(PARTS[:, 2, :, :], REST[:, :, :], PARTS[:, 1, :, :], ALU.subtract) \
                    .then_inc(part_made, 1)

            def causal(b, u):
                pool.wait_ge(exp_done, 12 * b + 2 * u + 2)
                px = PX[:, 6 * (b % 2) + u, :]
                if u % 3 < 2:
                    v, n = px.rearrange("p (h q) -> p h q", h=4)[:, :, 0:P], 4
                else:
                    v, n = px.rearrange("p (h q) -> p h q", h=8), 8
                pool.affine_select(out=v, in_=v, compare_op=ALU.is_ge, fill=0.0, base=0,
                                   pattern=[[0, n], [1, P]], channel_multiplier=-1).then_inc(mask_done, 1)

            for b in range(SLOTS):
                cosine(b)
                if b:
                    split(b)

            def add_decoder_bias():
                pool.wait_ge(in_vdec, 16)
                pool.wait_ge(dec_turned, 32)
                pool.tensor_tensor(UT[:, :, :], UT[:, :, :], BDEC, ALU.add).then_inc(ut_ready, 1)

            for s in range(B - 1):
                front = s + 3 < B
                if s == B - 2:
                    add_decoder_bias()
                for tick in range(12):
                    if tick == 5 and front:
                        cosine(s + 3)
                    if tick == 8 and front:
                        split(s + 3)
                    if tick % 2 == 1:
                        causal(s, tick // 2)
            for u in range(6):
                causal(B - 1, u)

            def split_hidden(p, n):
                i = 2 * p + n // 2
                pool.wait_ge(h_sb, 2 * (NF * p + n + 1))
                pool.tensor_tensor(HS[:, n, :], HS[:, n, :], HP[p % 2][:, n, 0, :], ALU.subtract) \
                    .then_inc(h_split, 1)
                pool.wait_ge(h_split, 3 * i + 1)
                pool.tensor_scalar(HP[p % 2][:, n, 1, :], HS[:, n, :], 1.0, 1.0, ALU.mult, ALU.mult) \
                    .then_inc(h_split, 1)
                pool.wait_ge(h_split, 3 * i + 2)
                pool.tensor_tensor(HP[p % 2][:, n, 2, :], HS[:, n, :], HP[p % 2][:, n, 1, :], ALU.subtract) \
                    .then_inc(h_split, 1)

            for p in range(LAST):
                for n in (1, 3):
                    split_hidden(p, n)

        @block.vector
        def _(dve):
            v = nc.vector
            dve.wait_ge(in_first, 32)
            dve.wait_ge(prep_psum, 1)
            v.tensor_scalar(STY[:, :], PIN[:, 0:B], float(W) ** -0.5, VEC[:, V_AFFB:V_AFFB + 1],
                            ALU.mult, ALU.add).then_inc(prep, 1)
            dve.wait_ge(prep, 1)
            v.tensor_tensor(STY2[:, :], STY[:, :], STY[:, :], ALU.mult).then_inc(prep, 1)
            v.tensor_tensor(WM2[:, :], WM[:, :], WM[:, :], ALU.mult).then_inc(prep, 1)
            dve.wait_ge(prep_psum, 2)
            v.tensor_scalar(DEM[:, 0, :], PSM[0][:, 0:B], 1e-8, None, ALU.add).then_inc(prep, 1)
            dve.wait_ge(prep_act, 1)
            v.reciprocal(DCO[:, :], DEM[:, 1, :]).then_inc(prep, 1)

            def set_rows(i):
                if i == 0:
                    dve.wait_ge(in_rows, 16)
                for S, R in ((QS, ROWSQ), (KS, ROWSK)):
                    v.tensor_copy(S[i][:, :, :].rearrange("p h (t q) -> p (h t) q", q=P),
                                  R[:, :].unsqueeze(1).to_broadcast([P, H * T, P])).then_inc(rows_set, 1)

            def clip(b):
                dve.wait_ge(y1_ready, b + 1)
                wait(dve, v_psum, b - 1)
                v.tensor_scalar(Y[:, b % 2, :], Y1[:, :], 256.0, -256.0, ALU.min, ALU.max) \
                    .then_inc(y_ready, 1)

            def rope_sine(b, side):
                if b == 0:
                    dve.wait_ge(in_rope, 16)
                dve.wait_ge(qk_sb, 2 * b + 2)
                wait(dve, rope_ready, b)
                a, o = (64, 0) if side == 0 else (0, 64)
                v.tensor_tensor(RS[o:o + 64, :, :], QK[a:a + 64, :, :],
                                ROPE[a:a + 64, 1, :].unsqueeze(1).to_broadcast([64, 2, L]), ALU.mult) \
                    .then_inc(rope_terms, 1)

            def rope_sum(b):
                dve.wait_ge(rope_terms, 2 * b + 2)
                dve.wait_ge(rope_cos, b + 1)
                wait(dve, part_made, 3 * (b - 1))
                v.tensor_tensor(RP[:, b % 2, :, :], RC[:, :, :], RS[:, :, :], ALU.add).then_inc(rope_ready, 1)

            def reduce_max(b, n):
                _, h0, nh, t = unit_of(n)
                dve.wait_ge(smax_psum, 12 * b + n + 1)
                if n == 0:
                    wait(dve, m_parts, 2 * (b - 1))
                v.tensor_reduce(MX[:, b % 2, t, h0:h0 + nh],
                                PSM[(12 * b + n) % 3][:, :].rearrange("p (h k) -> p h k", h=nh), AX.X, ALU.max) \
                    .then_inc(smax_read, 1)

            def split_max(b, half):
                dve.wait_ge(smax_read, 12 * b + 6 * half + 6)
                wait(dve, m_psum, 2 * (b - 1) + half + 1)
                mx = MX[:, b % 2, :, 8 * half:8 * half + 8]
                v.tensor_scalar(MP[:, half, :, 0, :], mx, -1.0, None, ALU.mult).then_inc(m_hi, 1)
                dve.wait_ge(m_hi, 2 * b + half + 1)
                v.scalar_tensor_tensor(out=MP[:, half, :, 1, :], in0=mx, scalar=-1.0,
                                       in1=MP[:, half, :, 0, :], op0=ALU.mult, op1=ALU.subtract) \
                    .then_inc(m_parts, 1)

            def normalise(b, t):
                dve.wait_ge(tr_psum, 2 * b + t + 1)
                wait(dve, at_psum, b)
                o = POUT[:, :].rearrange("p (h c) -> p h c", c=32)
                v.reciprocal(RL[:, t, :], o[:, :, D]).then_inc(rl_ready, 1)
                dve.wait_ge(rl_ready, 2 * b + t + 1)
                v.tensor_tensor(ON[:, t, :].rearrange("p (h d) -> p h d", d=D), o[:, :, 0:D],
                                RL[:, t, :].unsqueeze(2).to_broadcast([P, H, D]), ALU.mult) \
                    .then_inc(norm_done, 1)

            def residual(b):
                dve.wait_ge(wo_psum, b + 1)
                v.scalar_tensor_tensor(out=X1[:, b * L:(b + 1) * L], in0=POUT[:, L:2 * L],
                                       scalar=VEC[:, V_BO:V_BO + 1], in1=X[:, b * L:(b + 1) * L],
                                       op0=ALU.add, op1=ALU.add).then_inc(x1_ready, 1)

            def split_first():
                dve.wait_ge(part1_made, 1)
                v.tensor_tensor(REST[:, :, :], RP[:, 0, :, :], PARTS[:, 0, :, :], ALU.subtract) \
                    .then_inc(part_made, 1)
                dve.wait_ge(part_made, 1)
                v.tensor_copy(PARTS[:, 1, :, :], REST[:, :, :]).then_inc(part_made, 1)
                dve.wait_ge(part_made, 2)
                v.tensor_tensor(PARTS[:, 2, :, :], REST[:, :, :], PARTS[:, 1, :, :], ALU.subtract) \
                    .then_inc(part_made, 1)

            def take_weights():
                dve.wait_ge(wb_psum, 1)
                for i in range(2):
                    v.tensor_copy(WB[:, 4 * i:4 * i + 4, :], PWB[i][:, :].rearrange("p (b e) -> p b e", b=4)) \
                        .then_inc(wb_ready, 1)
                v.tensor_copy(BB[:, :], PWB[2][:, 0:B]).then_inc(wb_ready, 1)

            clip(0)
            set_rows(0)
            rope_sine(0, 0)
            rope_sine(0, 1)
            rope_sum(0)
            split_first()
            clip(1)
            rope_sine(1, 0)
            rope_sine(1, 1)
            rope_sum(1)
            clip(2)
            set_rows(1)
            rope_sine(2, 0)
            rope_sine(2, 1)
            rope_sum(2)
            for n in range(6):
                reduce_max(0, n)
            split_max(0, 0)
            for n in range(6, 12):
                reduce_max(0, n)
            for s in range(B - 1):
                front, tail = s + 3 < B, s > 0
                for tick in range(12):
                    if tick == 0:
                        split_max(s, 1)
                    if tick == 4 and front:
                        clip(s + 3)
                    if tick == 5 and tail:
                        normalise(s - 1, 0)
                    if tick == 6:
                        split_max(s + 1, 0)
                    if tick == 6 and tail:
                        normalise(s - 1, 1)
                    if tick == 6 and front:
                        rope_sine(s + 3, 0)
                        rope_sine(s + 3, 1)
                    if tick == 7 and front:
                        rope_sum(s + 3)
                    if tick == 9 and tail:
                        residual(s - 1)
                    reduce_max(s + 1, tick)

            def take_o2(p):
                dve.wait_ge(o2_psum, p + 1)
                if p == 0:
                    dve.wait_ge(o_psum, 2 * (B - 1))
                for i in range(2):
                    b = 2 * p + i
                    v.tensor_scalar(O2[:, p % 2, i * L:(i + 1) * L], PIN[:, i * L:(i + 1) * L],
                                    BB[:, b:b + 1], None, ALU.add).then_inc(o2_parts, 1)

            def split_o2(p):
                dve.wait_ge(o2_parts, 5 * p + 2)
                wait(dve, h_psum, NF * (p - 1))
                parts = O2P[:, p % 2]
                v.tensor_copy(parts[:, 0, :], O2[:, p % 2, :]).then_inc(o2_parts, 1)
                dve.wait_ge(o2_parts, 5 * p + 3)
                v.tensor_tensor(O2[:, p % 2, :], O2[:, p % 2, :], parts[:, 0, :], ALU.subtract) \
                    .then_inc(o2_parts, 1)
                dve.wait_ge(o2_parts, 5 * p + 4)
                v.tensor_copy(parts[:, 1, :], O2[:, p % 2, :]).then_inc(o2_left, 1)
                dve.wait_ge(o2_left, p + 1)
                v.tensor_tensor(parts[:, 2, :], O2[:, p % 2, :], parts[:, 1, :], ALU.subtract) \
                    .then_inc(o2_parts, 1)

            def hidden_rest(p, n):
                dve.wait_ge(h_sb, 2 * (NF * p + n + 1))
                v.tensor_tensor(HS[:, n, :], HS[:, n, :], HP[p % 2][:, n, 0, :], ALU.subtract) \
                    .then_inc(h_rest, 1)

            def third_part(p, n):
                dve.wait_ge(h_second, 2 * p + n // 2 + 1)
                v.tensor_tensor(HP[p % 2][:, n, 2, :], HS[:, n, :], HP[p % 2][:, n, 1, :], ALU.subtract) \
                    .then_inc(h_third, 1)

            def finish_last():
                for i in range(2):
                    dve.wait_ge(f_psum, LAST + 1 + i)
                    dst, at = slice(i * L, (i + 1) * L), (2 * LAST + i) * L
                    v.tensor_scalar(FT[:, LAST % 2, dst], PF[(LAST + i) % 2][:, 0:L], ALPHA[:, NF:NF + 1],
                                    VEC[:, V_B2:V_B2 + 1], ALU.mult, ALU.add).then_inc(f_scaled, 1)
                    dve.wait_ge(f_scaled, LAST + 1 + i)
                    dve.wait_ge(out_stored[LAST % 2], 16 * (LAST // 2))
                    v.tensor_tensor(OUT[:, LAST % 2, dst], FT[:, LAST % 2, dst], X1[:, at:at + L],
                                    ALU.add).then_inc(out_ready, 1)

            def finish(p):
                if p == 0:
                    dve.wait_ge(o_psum, 2 * B)
                dve.wait_ge(f_psum, p + 1)
                v.tensor_scalar(FT[:, p % 2, :], PF[p % 2][:, :], ALPHA[:, NF:NF + 1],
                                VEC[:, V_B2:V_B2 + 1], ALU.mult, ALU.add).then_inc(f_scaled, 1)
                dve.wait_ge(f_scaled, p + 1)
                wait(dve, out_stored[p % 2], 16 * (p // 2))
                v.tensor_tensor(OUT[:, p % 2, :], FT[:, p % 2, :], X1[:, 2 * L * p:2 * L * (p + 1)],
                                ALU.add).then_inc(out_ready, 1)

            split_max(B - 1, 1)
            take_weights()
            normalise(B - 2, 0)
            take_o2(0)
            normalise(B - 2, 1)
            split_o2(0)
            residual(B - 2)
            take_o2(1)
            split_o2(1)
            hidden_rest(0, 0)
            take_o2(2)
            hidden_rest(0, 2)
            third_part(0, 0)
            normalise(B - 1, 0)
            split_o2(2)
            normalise(B - 1, 1)
            third_part(0, 2)
            hidden_rest(1, 0)
            hidden_rest(1, 2)
            residual(B - 1)
            third_part(1, 0)
            third_part(1, 2)
            take_o2(3)
            hidden_rest(2, 0)
            split_o2(3)
            hidden_rest(2, 2)
            finish(0)
            third_part(2, 0)
            third_part(2, 2)
            finish(1)
            finish(2)
            finish_last()


def kernel(**inputs):
    import numpy as np
    import concourse.bacc as bacc
    from concourse.bass_utils import run_bass_kernel_spmd as run

    a = {k: np.asarray(v) for k, v in inputs.items()}
    bf = np.dtype("bfloat16")

    order = np.arange(C).reshape(H, D).T.reshape(-1)
    wq, wk = a["L0_attn_Wq"][order], a["L0_attn_Wk"][order]

    theta = np.float32(1250) ** (np.float32(-2.0) * np.arange(D // 2, dtype=np.float32) / np.float32(D))
    theta = np.concatenate([theta, theta]).astype(np.float32)
    angle = np.arange(1, L + 1, dtype=np.float32)[None, :] * np.repeat(theta, H)[:, None]
    sign = np.where(np.arange(C) < C // 2, 1.0, -1.0).astype(np.float32)[:, None]
    rope = np.stack([np.cos(angle), sign * np.sin(angle)], axis=1).astype(np.float32)
    rowsq, rowsk = np.zeros((P, P)), np.zeros((P, P))
    rowsk[MROW:MROW + 2] = 1.0
    i = np.arange(P)
    for r in range(32):
        rowsq[MASK0 + r] = np.where(i // 4 == r, 2.0 ** (-42.0 * (i % 4)), 0.0)
        rowsk[MASK0 + r] = np.where(i // 4 == r, -(2.0 ** (-12 + 42.0 * (i % 4))), 0.0)
    for r in range(1, 32):
        rowsq[MASK0 + 31 + r] = i // 4 < r
        rowsk[MASK0 + 31 + r] = np.where(i // 4 == r, -(2.0 ** 60), 0.0)

    col = lambda v: v.reshape(-1, P).T
    vecs = np.concatenate([col(a["L0_cond_bias"]), col(a["L0_cond_affine_b"]), col(a["L0_attn_bq"][order]),
                           col(a["L0_attn_bk"][order]), col(a["L0_attn_bv"]), col(a["L0_attn_bo"]),
                           col(a["L0_ffn_b2"]), col(a["L0_ffn_b1"])], axis=1)
    condaff = np.zeros((2 * W, 2 * B + C), np.float32)
    condaff[:W, :B] = condaff[W:, B:2 * B] = a["cond_512"].T
    condaff[:W, 2 * B:] = a["L0_cond_affine_w"].T
    bdec = np.broadcast_to(a["L0_cond2_b_dec"].reshape(C + 1, K).T[:, None], (K, B, C + 1))
    arrays = {
        "xT": a["x"].reshape(B * L, C).T,
        "condaff": condaff,
        "wvecs": np.concatenate([vecs, a["L0_cond_weight"].T], axis=1),
        "wqkvT": np.concatenate([wq, wk, a["L0_attn_Wv"]], axis=0).T,
        "rope": rope,
        "rowsb": np.stack([rowsq, rowsk, np.eye(P)], axis=1).astype(bf),
        "wdec": a["L0_cond2_W_dec"].reshape(W, C + 1, 2, K // 2).transpose(2, 0, 3, 1).reshape(2 * W, UC),
        "mats": np.concatenate([np.eye(P, dtype=np.float32), a["L0_attn_Wo"].T], axis=1),
        "vdec": np.concatenate([a["L0_cond2_V"], bdec.reshape(K, -1)], axis=1),
        "w12": np.stack([a["L0_ffn_w1"].T, a["L0_ffn_w2"].T.reshape(NF, P, C).transpose(1, 0, 2)
                         .reshape(P, F)], axis=1),
        "w12n": np.stack([a["L0_ffn_w1"].reshape(NF, P, C).transpose(1, 0, 2).reshape(P, F),
                          a["L0_ffn_w2"]], axis=1),
        "zeros2": np.zeros((2, H, L), bf),
    }
    arrays = {k: np.ascontiguousarray(v) for k, v in arrays.items()}
    nc = bacc.Bacc("TRN2", target_bir_lowering=False, num_devices=1)
    args = [nc.dram_tensor(k, v.shape, mybir.dt.from_np(v.dtype), kind="ExternalInput").ap()
            for k, v in arrays.items()]
    out = nc.dram_tensor("outT", (C, B * L), F32, kind="ExternalOutput").ap()
    build(nc, *args, out)
    r = run(nc, [arrays], core_ids=[0])
    return r.results[0]["outT"].T.reshape(B, L, C)
```
